# Optimizing a Trainium2 kernel written in Bass

```python
import numpy as np
import jax
import jax.numpy as jnp

def _softmax(x, axis=-1):
    return jax.nn.softmax(x, axis=axis)

def _gelu(x):
    return jax.nn.gelu(x, approximate=True)

def _silu(x):
    return jax.nn.silu(x)

def _sigmoid(x):
    return jax.nn.sigmoid(x)

def _layernorm(x, axis=-1, eps=1e-05):
    m = jnp.mean(x, axis=axis, keepdims=True)
    v = jnp.var(x, axis=axis, keepdims=True)
    return (x - m) / jnp.sqrt(v + eps)

def _scatter_add(tgt, idx, src, axis=0):
    return tgt.at[idx].add(src)

def _segment_sum(src, seg, n):
    return jax.ops.segment_sum(src, seg, n)
kernel_name = 'mk_hybrid_d1_jaxref_r4_5f2d97'

def setup_inputs(seed: int=0):
    np.random.seed(seed)
    _w = jnp.asarray

    def _L0_attn_a_setup():
        import jax, jax.numpy as jnp
        import numpy as np
        N_HEADS = 16
        EPS = 1e-06
        key = jax.random.key(seed)
        ks = jax.random.split(key, 10)
        B, T, D = (2, 512, 256)
        x = jax.random.normal(ks[0], (B, T, D), dtype=jnp.float32)
        norm_w = jnp.ones((D,), dtype=jnp.float32)
        bound = float(np.sqrt(6.0 / (D + D)))

        def lin(k):
            return jax.random.uniform(k, (D, D), dtype=jnp.float32, minval=-bound, maxval=bound)
        Wq, Wk, Wv, Wo = (lin(ks[1]), lin(ks[2]), lin(ks[3]), lin(ks[4]))
        bq = jnp.zeros((D,), dtype=jnp.float32)
        bk = jnp.zeros((D,), dtype=jnp.float32)
        bv = jnp.zeros((D,), dtype=jnp.float32)
        bo = jnp.zeros((D,), dtype=jnp.float32)
        return {'x': x, 'norm_w': norm_w, 'Wq': Wq, 'bq': bq, 'Wk': Wk, 'bk': bk, 'Wv': Wv, 'bv': bv, 'Wo': Wo, 'bo': bo}
    _L0_attn_a_in = _L0_attn_a_setup()

    def _L0_attn_b_setup():
        import jax, jax.numpy as jnp
        import numpy as np
        D, STATE, CONV = (256, 16, 4)
        B_, L_ = (8, 512)

        def _ssm_forward(x, conv_w, conv_b, Wd, bd, Wb, Wc, log_a, Wg, bg, Wo, bo):
            b, l, d = x.shape
            xt = jnp.transpose(x, (0, 2, 1))
            xc = jax.lax.conv_general_dilated(xt, conv_w, window_strides=(1,), padding=[(CONV - 1, 0)], feature_group_count=d, dimension_numbers=('NCH', 'OIH', 'NCH'))
            xc = jnp.transpose(xc + conv_b[None, :, None], (0, 2, 1))
            xc = jax.nn.silu(xc)
            delta = jax.nn.softplus(jnp.einsum('bld,ed->ble', xc, Wd) + bd)
            Bm = jnp.einsum('bld,nd->bln', xc, Wb)
            Cm = jnp.einsum('bld,nd->bln', xc, Wc)
            A = -jnp.exp(log_a)

            def step(h, inputs):
                dt, bt, ct, xt_ = inputs
                decay = jnp.exp(A[None] * dt[:, :, None])
                inp = dt[:, :, None] * xt_[:, :, None] * bt[:, None, :]
                h = decay * h + inp
                y = jnp.einsum('bdn,bn->bd', h, ct)
                return (h, y)
            h0 = jnp.zeros((b, d, STATE), dtype=x.dtype)
            seq = (jnp.moveaxis(delta, 1, 0), jnp.moveaxis(Bm, 1, 0), jnp.moveaxis(Cm, 1, 0), jnp.moveaxis(xc, 1, 0))
            _, ys = jax.lax.scan(step, h0, seq)
            y = jnp.moveaxis(ys, 0, 1)
            gate = jax.nn.sigmoid(jnp.einsum('bld,ed->ble', x, Wg) + bg)
            return jnp.einsum('bld,ed->ble', y * gate, Wo) + bo
        key = jax.random.key(seed)
        ks = jax.random.split(key, 12)
        s = 0.02
        return {'x': jax.random.normal(ks[0], (B_, L_, D), dtype=jnp.float32), 'conv_w': jax.random.normal(ks[1], (D, 1, CONV), dtype=jnp.float32) * s, 'conv_b': jnp.zeros((D,), dtype=jnp.float32), 'Wd': jax.random.normal(ks[2], (D, D), dtype=jnp.float32) * s, 'bd': jnp.zeros((D,), dtype=jnp.float32), 'Wb': jax.random.normal(ks[3], (STATE, D), dtype=jnp.float32) * s, 'Wc': jax.random.normal(ks[4], (STATE, D), dtype=jnp.float32) * s, 'log_a': jnp.log(jnp.tile(jnp.linspace(1.0, STATE, STATE, dtype=jnp.float32), (D, 1))), 'Wg': jax.random.normal(ks[5], (D, D), dtype=jnp.float32) * s, 'bg': jnp.zeros((D,), dtype=jnp.float32), 'Wo': jax.random.normal(ks[6], (D, D), dtype=jnp.float32) * s, 'bo': jnp.zeros((D,), dtype=jnp.float32)}
    _L0_attn_b_in = _L0_attn_b_setup()

    def _L0_ffn_setup():
        import jax, jax.numpy as jnp
        import numpy as np
        B, S, D = (8, 1024, 256)
        E, R, K = (6, 16, 2)
        key = jax.random.key(seed)
        ks = jax.random.split(key, 9)
        sc = 0.02
        return {'x': jax.random.normal(ks[0], (B, S, D), jnp.float32), 'base_W': jax.random.normal(ks[1], (D, D), jnp.float32) * sc, 'base_b': jax.random.normal(ks[2], (D,), jnp.float32) * sc, 'shared_A': jax.random.normal(ks[3], (R, D), jnp.float32) * sc, 'shared_B': jax.random.normal(ks[4], (D, R), jnp.float32) * sc, 'routed_A': jax.random.normal(ks[5], (E, R, D), jnp.float32) * sc, 'routed_B': jax.random.normal(ks[6], (E, D, R), jnp.float32) * sc, 'router_W': jax.random.normal(ks[7], (E, D), jnp.float32) * sc, 'router_b': jax.random.normal(ks[8], (E,), jnp.float32) * sc}
    _L0_ffn_in = _L0_ffn_setup()
    _d = {'L0_attn_a_x': _L0_attn_a_in['x'], 'L0_attn_a_norm_w': _L0_attn_a_in['norm_w'], 'L0_attn_a_Wq': _L0_attn_a_in['Wq'], 'L0_attn_a_bq': _L0_attn_a_in['bq'], 'L0_attn_a_Wk': _L0_attn_a_in['Wk'], 'L0_attn_a_bk': _L0_attn_a_in['bk'], 'L0_attn_a_Wv': _L0_attn_a_in['Wv'], 'L0_attn_a_bv': _L0_attn_a_in['bv'], 'L0_attn_a_Wo': _L0_attn_a_in['Wo'], 'L0_attn_a_bo': _L0_attn_a_in['bo'], 'L0_attn_b_conv_w': _L0_attn_b_in['conv_w'], 'L0_attn_b_conv_b': _L0_attn_b_in['conv_b'], 'L0_attn_b_Wd': _L0_attn_b_in['Wd'], 'L0_attn_b_bd': _L0_attn_b_in['bd'], 'L0_attn_b_Wb': _L0_attn_b_in['Wb'], 'L0_attn_b_Wc': _L0_attn_b_in['Wc'], 'L0_attn_b_log_a': _L0_attn_b_in['log_a'], 'L0_attn_b_Wg': _L0_attn_b_in['Wg'], 'L0_attn_b_bg': _L0_attn_b_in['bg'], 'L0_attn_b_Wo': _L0_attn_b_in['Wo'], 'L0_attn_b_bo': _L0_attn_b_in['bo'], 'L0_ffn_base_W': _L0_ffn_in['base_W'], 'L0_ffn_base_b': _L0_ffn_in['base_b'], 'L0_ffn_shared_A': _L0_ffn_in['shared_A'], 'L0_ffn_shared_B': _L0_ffn_in['shared_B'], 'L0_ffn_routed_A': _L0_ffn_in['routed_A'], 'L0_ffn_routed_B': _L0_ffn_in['routed_B'], 'L0_ffn_router_W': _L0_ffn_in['router_W'], 'L0_ffn_router_b': _L0_ffn_in['router_b']}
    _x0 = _d['L0_attn_a_x']
    _d['L0_attn_a_x'] = jax.random.normal(jax.random.fold_in(jax.random.key(seed), 1), (16, 512, 256), dtype=_x0.dtype)
    del _x0
    return _d

def reference(L0_attn_a_x, L0_attn_a_norm_w, L0_attn_a_Wq, L0_attn_a_bq, L0_attn_a_Wk, L0_attn_a_bk, L0_attn_a_Wv, L0_attn_a_bv, L0_attn_a_Wo, L0_attn_a_bo, L0_attn_b_conv_w, L0_attn_b_conv_b, L0_attn_b_Wd, L0_attn_b_bd, L0_attn_b_Wb, L0_attn_b_Wc, L0_attn_b_log_a, L0_attn_b_Wg, L0_attn_b_bg, L0_attn_b_Wo, L0_attn_b_bo, L0_ffn_base_W, L0_ffn_base_b, L0_ffn_shared_A, L0_ffn_shared_B, L0_ffn_routed_A, L0_ffn_routed_B, L0_ffn_router_W, L0_ffn_router_b):

    def _L0_attn_a_ref(x, norm_w, Wq, bq, Wk, bk, Wv, bv, Wo, bo):
        import jax, jax.numpy as jnp
        import numpy as np
        N_HEADS = 16
        EPS = 1e-06
        B, T, D = x.shape
        H = N_HEADS
        hd = D // H
        xn = x * jax.lax.rsqrt(jnp.mean(x * x, axis=-1, keepdims=True) + EPS) * norm_w
        q = (xn @ Wq.T + bq).reshape(B, T, H, hd).transpose(0, 2, 1, 3)
        k = (xn @ Wk.T + bk).reshape(B, T, H, hd).transpose(0, 2, 1, 3)
        v = (xn @ Wv.T + bv).reshape(B, T, H, hd).transpose(0, 2, 1, 3)
        scale = 1.0 / jnp.sqrt(jnp.asarray(hd, dtype=x.dtype))
        scores = jnp.einsum('bhqd,bhkd->bhqk', q, k) * scale
        causal = jnp.triu(jnp.ones((T, T), dtype=bool), k=1)
        scores = jnp.where(causal, jnp.asarray(-jnp.inf, dtype=scores.dtype), scores)
        attn = jax.nn.softmax(scores, axis=-1)
        out = jnp.einsum('bhqk,bhkd->bhqd', attn, v)
        out = out.transpose(0, 2, 1, 3).reshape(B, T, D)
        out = out @ Wo.T + bo
        return xn + out

    def _L0_attn_b_ref(x, conv_w, conv_b, Wd, bd, Wb, Wc, log_a, Wg, bg, Wo, bo):
        import jax, jax.numpy as jnp
        import numpy as np
        D, STATE, CONV = (256, 16, 4)
        B_, L_ = (8, 512)

        def _ssm_forward(x, conv_w, conv_b, Wd, bd, Wb, Wc, log_a, Wg, bg, Wo, bo):
            b, l, d = x.shape
            xt = jnp.transpose(x, (0, 2, 1))
            xc = jax.lax.conv_general_dilated(xt, conv_w, window_strides=(1,), padding=[(CONV - 1, 0)], feature_group_count=d, dimension_numbers=('NCH', 'OIH', 'NCH'))
            xc = jnp.transpose(xc + conv_b[None, :, None], (0, 2, 1))
            xc = jax.nn.silu(xc)
            delta = jax.nn.softplus(jnp.einsum('bld,ed->ble', xc, Wd) + bd)
            Bm = jnp.einsum('bld,nd->bln', xc, Wb)
            Cm = jnp.einsum('bld,nd->bln', xc, Wc)
            A = -jnp.exp(log_a)

            def step(h, inputs):
                dt, bt, ct, xt_ = inputs
                decay = jnp.exp(A[None] * dt[:, :, None])
                inp = dt[:, :, None] * xt_[:, :, None] * bt[:, None, :]
                h = decay * h + inp
                y = jnp.einsum('bdn,bn->bd', h, ct)
                return (h, y)
            h0 = jnp.zeros((b, d, STATE), dtype=x.dtype)
            seq = (jnp.moveaxis(delta, 1, 0), jnp.moveaxis(Bm, 1, 0), jnp.moveaxis(Cm, 1, 0), jnp.moveaxis(xc, 1, 0))
            _, ys = jax.lax.scan(step, h0, seq)
            y = jnp.moveaxis(ys, 0, 1)
            gate = jax.nn.sigmoid(jnp.einsum('bld,ed->ble', x, Wg) + bg)
            return jnp.einsum('bld,ed->ble', y * gate, Wo) + bo
        return _ssm_forward(x, conv_w, conv_b, Wd, bd, Wb, Wc, log_a, Wg, bg, Wo, bo)

    def _L0_ffn_ref(x, base_W, base_b, shared_A, shared_B, routed_A, routed_B, router_W, router_b):
        import jax, jax.numpy as jnp
        import numpy as np
        B, S, D = (8, 1024, 256)
        E, R, K = (6, 16, 2)
        base_out = jax.lax.stop_gradient(jnp.einsum('bsi,oi->bso', x, base_W) + base_b)
        shared_out = jnp.einsum('bsr,or->bso', jnp.einsum('bsi,ri->bsr', x, shared_A), shared_B)
        logits = jnp.einsum('bsi,ei->bse', x, router_W) + router_b
        gate = jax.nn.softmax(logits, axis=-1)
        topk_w, topk_i = jax.lax.top_k(gate, K)
        sparse_w = jnp.sum(jax.nn.one_hot(topk_i, E, dtype=gate.dtype) * topk_w[..., None], axis=-2)
        sparse_w = sparse_w / (jnp.sum(sparse_w, axis=-1, keepdims=True) + 1e-06)
        h = jnp.einsum('bsi,eri->bser', x, routed_A)
        routed_outs = jnp.einsum('bser,eor->bseo', h, routed_B)
        routed_out = jnp.einsum('bseo,bse->bso', routed_outs, sparse_w)
        return base_out + shared_out + routed_out
    x = L0_attn_a_x
    x = x + _L0_attn_a_ref(_layernorm(x, axis=-1), L0_attn_a_norm_w, L0_attn_a_Wq, L0_attn_a_bq, L0_attn_a_Wk, L0_attn_a_bk, L0_attn_a_Wv, L0_attn_a_bv, L0_attn_a_Wo, L0_attn_a_bo)
    x = x + _L0_ffn_ref(_layernorm(x, axis=-1), L0_ffn_base_W, L0_ffn_base_b, L0_ffn_shared_A, L0_ffn_shared_B, L0_ffn_routed_A, L0_ffn_routed_B, L0_ffn_router_W, L0_ffn_router_b)
    x = x + _L0_attn_b_ref(_layernorm(x, axis=-1), L0_attn_b_conv_w, L0_attn_b_conv_b, L0_attn_b_Wd, L0_attn_b_bd, L0_attn_b_Wb, L0_attn_b_Wc, L0_attn_b_log_a, L0_attn_b_Wg, L0_attn_b_bg, L0_attn_b_Wo, L0_attn_b_bo)
    x = x + _L0_ffn_ref(_layernorm(x, axis=-1), L0_ffn_base_W, L0_ffn_base_b, L0_ffn_shared_A, L0_ffn_shared_B, L0_ffn_routed_A, L0_ffn_routed_B, L0_ffn_router_W, L0_ffn_router_b)
    return x

_drawn_inputs = setup_inputs


def setup_inputs(seed=0):
    import zlib

    import numpy as np

    out = dict(_drawn_inputs(seed))
    spreads = {'L0_attn_a_norm_w': (1.0, 0.2),
     'L0_attn_a_bq': (0.0, 0.8),
     'L0_attn_a_bk': (0.0, 2.0),
     'L0_attn_a_bv': (0.0, 0.1),
     'L0_attn_a_bo': (0.0, 0.1),
     'L0_attn_b_conv_b': (0.0, 0.8),
     'L0_attn_b_bd': (0.0, 0.8),
     'L0_attn_b_bg': (0.0, 0.8),
     'L0_attn_b_bo': (0.0, 0.345)}
    factors = {'L0_attn_b_conv_w': 8.0,
     'L0_attn_b_Wd': 8.0,
     'L0_attn_b_Wb': 8.0,
     'L0_attn_b_Wc': 8.0,
     'L0_attn_b_log_a': 8.0,
     'L0_attn_b_Wg': 8.0,
     'L0_attn_b_Wo': 8.0,
     'L0_ffn_base_b': 2.968,
     'L0_ffn_routed_A': 3.436,
     'L0_ffn_routed_B': 3.431,
     'L0_ffn_router_W': 4.268,
     'L0_ffn_router_b': 8.0,
     'L0_ffn_shared_A': 3.297,
     'L0_ffn_shared_B': 3.212}
    for name, (base, spread) in spreads.items():
        noise = np.random.default_rng([zlib.crc32(name.encode()), seed]).standard_normal(out[name].shape)
        drawn = base * np.exp(spread * noise) if base else spread * noise
        out[name] = jnp.asarray(drawn.astype(out[name].dtype))
    for name, factor in factors.items():
        out[name] = (out[name] * factor).astype(out[name].dtype)
    return out
```

```python
from contextlib import ExitStack

import concourse.bass as bass
from concourse import mybir

F32 = mybir.dt.float32
BF16 = mybir.dt.bfloat16
ALU = mybir.AluOpType
ACT = mybir.ActivationFunctionType
AXX = mybir.AxisListType.X

P = 128
BIG = -1.0e30


class Tally:

    def __init__(self, sem, per, credit=0, step=1):
        self.sem, self.per, self.credit, self.step = sem, per, credit, step
        self.n = 0

    def at(self, b, n):
        return b * (self.per * self.step) + (n * self.step + self.credit)

    def next(self, b):
        self.n += 1
        return self.at(b, (self.n - 1) % self.per + 1)


def hybrid_block(nc, x, norm_w, wqk_t, bqk_c, wv_t, bv, wo_t, bo, conv_w, conv_b, wd_t, bd, wbc_t,
                 log_a, wg_t, bg, wso_t, bso, base_t, base_b, down_t, up_s, router_b, out):
    NB, T, D = x.shape
    C = D // P
    TB = T // P
    H = 16
    HD = D // H
    NS = log_a.shape[1]
    E = router_b.shape[0]
    R = up_s.shape[0] // (E + 1)
    LR = down_t.shape[1]
    HP = H // 2
    UN = 5
    TAPS = conv_w.shape[1]
    TERMS = [(0, 0), (0, 1), (1, 0), (0, 2), (2, 0), (1, 1)]
    KS = len(TERMS) * HD

    ctx = ExitStack()
    with ctx:
        def sb(name, shape, dt=F32):
            return ctx.enter_context(nc.sbuf_tensor(name, shape, dt))

        def sem(name):
            return ctx.enter_context(nc.semaphore(name))

        def tally(name, per, credit=0, step=1):
            t = Tally(sem(name), per, credit, step)
            tallies.append(t)
            return t

        tallies = []
        bank = [ctx.enter_context(nc.psum_tensor(f"bank{i}", [P, 512], F32)) for i in range(8)]

        ident = sb("ident", [P, P])
        ident_bf = sb("ident_bf", [P, P], BF16)
        mask_qk = sb("mask_qk", [P, P], BF16)
        mask_kq = sb("mask_kq", [P, P], BF16)
        onehot = sb("onehot", [3 * 2 * NS, 2 * NS, P], BF16)
        wqk = sb("wqk", [P, C, 2 * D])
        wv = sb("wv", [P, C, D])
        wo = sb("wo", [P, C, D])
        wd = sb("wd", [P, C, D])
        wg = sb("wg", [P, C, D])
        wso = sb("wso", [P, C, D])
        wbase = sb("wbase", [P, C, D])
        wdown = sb("wdown", [P, C, LR])
        wup = sb("wup", [(E + 1) * R, D])
        wbc = sb("wbc", [P, C, 3, 2 * NS])
        bqk = sb("bqk", [P, 2 * C])
        bd_c = sb("bd_c", [P, C])
        bg_c = sb("bg_c", [P, C])
        cw = sb("cw", [P, C, TAPS])
        cb = sb("cb", [P, C])
        a_neg = sb("a_neg", [P, C, NS])
        w_row = sb("w_row", [P, D])
        bv_row = sb("bv_row", [P, D])
        bo_row = sb("bo_row", [P, D])
        bso_row = sb("bso_row", [P, D])
        bb_row = sb("bb_row", [P, D])
        rb_row = sb("rb_row", [P, E])
        below = sb("below", [P, E, E])
        half = sb("half", [P, TB])

        x_in = sb("x_in", [P, TB, D])
        res_a = sb("res_a", [P, TB, D])
        res_s = sb("res_s", [P, TB, D])
        tok = sb("tok", [P, TB, D])
        xn = sb("xn", [P, TB, D])
        ao = xn
        hw = xn[:, 0:2, :].rearrange("p a d -> p (a d)")[:, 0:TB * (E + 1) * R].rearrange("p (t f) -> p t f", t=TB)
        hw_t = xn[0:(E + 1) * R, 2:4, :].rearrange("p a d -> p (a d)")
        xt = sb("xt", [P, C, T])
        pt = sb("pt", [P, 2 * UN * 512])
        pt_v = pt[:, :].rearrange("p (r u n) -> p r u n", r=2, u=UN)
        qkf = pt[:, 0:2 * C * T].rearrange("p (g t) -> p g t", g=2 * C)
        parts = pt[:, 2 * C * T:5 * C * T].bitcast(BF16).rearrange("p (j g t) -> p j g t", j=3, g=2 * C)
        sq = sb("sq", [KS + 2, H, T], BF16)
        sk = sb("sk", [KS + 2, H, T], BF16)
        v_sb = sb("v_sb", [P, TB, H, HD + 1])
        mxp = sb("mxp", [P, HP, UN, TB])
        negm = sb("negm", [P, TB, H])
        mrow = sb("mrow", [H, 2, T], BF16)
        rc = sb("rc", [P, 2 * TB])
        st = sb("st", [P, TB, 6])
        mv = sb("mv", [P, TB, 2])
        va = sb("va", [P, TB])
        rs = sb("rs", [P, TB])
        nm = sb("nm", [P, TB])
        lg = sb("lg", [P, TB, E])
        ex = sb("ex", [P, TB, E])
        cmp_a = sb("cmp_a", [P, TB, E, E])
        cmp_b = sb("cmp_b", [P, TB, E, E])
        rank = sb("rank", [P, TB, E])
        red = sb("red", [P, 4, TB])
        wts = sb("wts", [P, TB, E + 1])
        xs_t = sb("xs_t", [P, C, TAPS - 1 + T])
        xc = sb("xc", [P, C, T])
        sp_t = sb("sp_t", [P, C, T])
        dt = sb("dt", [P, C, T])
        u = sb("u", [P, C, T])
        gate = sb("gate", [P, C, T])
        bcs = sb("bcs", [3 * 2 * NS, T], BF16)
        bcr = sb("bcr", [3 * 2 * NS, T])
        b_all = sb("b_all", [P, NS, T])
        dec = sb("dec", [P, 2, C, T])
        inp = sb("inp", [P, 2, C, T])
        hc = sb("hc", [P, 2, C, T])

        scratch = nc.dram_tensor("qk_parts", [NB, 3, 2 * C, P, T], BF16, kind="Internal").ap()

        w_in = sem("weights_loaded")
        pool_const = sem("pool_constants")
        dve_const = sem("dve_constants")
        act_const = sem("act_constants")
        dve_const_step = sem("dve_constant_step")
        pool_const_step = sem("pool_constant_steps")
        waited = sem("waited")

        x_loaded = tally("x_loaded", 1, step=16)
        x_used = tally("x_used", 1, credit=1)
        var_a, rs_a = tally("attn_variance", 1), tally("attn_rsqrt", 1)
        xhat_a = tally("attn_normalised", 1)
        xn_done = tally("xn_done", 1)
        res_done = tally("res_done", 1)
        xn_turned = tally("xn_turned", C)
        xnt_done = tally("xnt_done", C)
        qk_ready = tally("qk_ready", 2 * C)
        qk_biased = tally("qk_biased", 2 * C)
        v_ready = tally("v_ready", 2)
        v_done = tally("v_done", 2)
        part_done = tally("part_done", 3)
        part_stored = tally("part_stored", 3, step=16)
        stacked = tally("stacked", 2 * len(TERMS), step=16)
        mx_ready = tally("scores_for_max", HP * UN + 1)
        mx_used = tally("scores_for_max_used", HP * UN + 2, credit=2)
        negm_done = tally("negm_done", 1)
        mrow_done = tally("mrow_done", 1)
        m_stacked = tally("max_stacked", 2, step=16)
        st_ready = tally("scores_ready", HP * UN)
        exp_done = tally("exp_done", HP * UN, credit=2)
        pv_ready = tally("pv_ready", HP, credit=2)
        pv_used = tally("pv_used", HP, credit=1)
        ao_turned = tally("ao_turned", C)
        aot_done = tally("aot_done", C)
        wo_ready = tally("wo_ready", 2)
        x1_done = tally("x1_done", 2)
        var_f, rs_f = tally("ffn_variance", 2), tally("ffn_rsqrt", 2)
        xhat_f = tally("ffn_normalised", 2)
        bias_f = tally("ffn_bias_added", 2)
        f_turned = tally("ffn_turned", 2 * C)
        ft_done = tally("ffn_turned_copied", 2 * C)
        low_ready = tally("low_rank_ready", 2)
        lg_done = tally("logits_done", 2)
        ex_done = tally("router_exp_done", 2)
        hw_done = tally("weighted_low_rank", 2)
        hw_turned = tally("low_rank_turned", 2)
        hwt_done = tally("low_rank_copied", 2)
        f_ready = tally("ffn_ready", 4)
        f_done = tally("ffn_done", 4)
        x_stored = tally("x_stored", 1, credit=16, step=16)
        var_s, rs_s = tally("ssm_variance", 1), tally("ssm_rsqrt", 1)
        xhat_s = tally("ssm_normalised", 1)
        bias_s = tally("ssm_bias_added", 1)
        s_turned = tally("ssm_turned", C)
        xst_done = tally("xst_done", C)
        conv_done = tally("conv_done", C)
        tanh_done = tally("tanh_done", C)
        xc_done = tally("xc_done", C)
        g_ready = tally("gate_ready", C)
        g_done = tally("gate_done", C)
        d_ready = tally("delta_ready", C)
        sp_done = tally("softplus_parts", 1)
        u_done = tally("u_done", 2)
        bc_ready = tally("bc_ready", 1)
        bc_high = tally("bc_high", 1)
        bc_done = tally("bc_done", 1)
        b_ready = tally("b_spread", NS)
        b_done = tally("b_copied", NS, credit=2)
        dec_ready = tally("decay_ready", NS)
        inp_ready = tally("input_ready", NS)
        scan_done = tally("scan_done", NS, credit=2)
        c_ready = tally("c_spread", NS)
        hc_done = tally("hc_done", NS, credit=1)
        y_ready = tally("y_summed", NS, credit=2)
        y_done = tally("y_copied", 2)
        y_turned = tally("y_turned", C)
        yg_done = tally("gated_y", C)
        so_ready = tally("ssm_out_ready", 2)
        x3_done = tally("x3_done", 2)
        dve_a = tally("dve_attn_steps", 3)
        pool_a = tally("pool_attn_steps", 1)
        dve_m = tally("dve_max_steps", 1)
        dve_h = tally("dve_head_steps", HP)
        dve_f = tally("dve_ffn_steps", 2 * 14)
        dve_s = tally("dve_ssm_steps", 3 + TAPS - 1 + 2)
        act_s = tally("act_ssm_steps", 2)

        block = ctx.enter_context(nc.Block())

        def rows(t, n=TB):
            return t[:, None, :].to_broadcast([P, n, D])

        def turn(src, dst, c):
            for tb in range(TB):
                last = nc.tensor.transpose(dst[:, tb * P:(tb + 1) * P], src[:, tb, c * P:(c + 1) * P], ident[:, :])
            return last

        N_LOADS = 24

        @block.sync
        def _(sp):
            def chunked(w):
                return w.rearrange("(c p) n -> p c n", p=P)

            loads = [
                (wqk[:, :, :], chunked(wqk_t)), (wv[:, :, :], chunked(wv_t)), (wo[:, :, :], chunked(wo_t)),
                (wd[:, :, :], chunked(wd_t)), (wg[:, :, :], chunked(wg_t)), (wso[:, :, :], chunked(wso_t)),
                (wbase[:, :, :], chunked(base_t)), (wdown[:, :, :], chunked(down_t)), (wup[:, :], up_s),
                (bqk[:, :], bqk_c), (bd_c[:, :], bd), (bg_c[:, :], bg),
                (cw[:, :, :], chunked(conv_w)), (cb[:, :], conv_b), (a_neg[:, :, :], chunked(log_a)),
            ]
            loads += [(wbc[:, :, j, :], chunked(wbc_t)) for j in range(3)]
            loads += [(t[:, :], v[None, :].to_broadcast([P, v.shape[0]])) for t, v in
                      ((w_row, norm_w), (bv_row, bv), (bo_row, bo), (bso_row, bso), (bb_row, base_b), (rb_row, router_b))]
            assert len(loads) == N_LOADS
            for dst, src in loads:
                sp.dma_start(dst, src).then_inc(w_in, 16)
            sp.sem_inc(x_stored.sem, 16)
            with sp.Fori(0, NB) as b:
                sp.wait_ge(x_used.sem, x_used.at(b, 0))
                sp.dma_start(x_in[:, :, :], x[b].rearrange("(t p) d -> p t d", p=P)).then_inc(x_loaded.sem, 16)
                for j in range(3):
                    sp.wait_ge(part_done.sem, part_done.at(b, j + 1))
                    sp.dma_start(scratch[b, j].rearrange("g p t -> p g t"), parts[:, j, :, :]).then_inc(part_stored.sem, 16)
                sp.wait_ge(part_stored.sem, part_stored.at(b, 3))
                for s, (jq, jk) in enumerate(TERMS):
                    for dst, j, g in ((sq, jq, 0), (sk, jk, C)):
                        src = scratch[b, j, g:g + C].rearrange("g (h i) t -> i (g h) t", i=HD)
                        sp.dma_start(dst[s * HD:(s + 1) * HD, :, :], src).then_inc(stacked.sem, 16)
                sp.wait_ge(mrow_done.sem, mrow_done.at(b, 1))
                for r in range(2):
                    sp.dma_start(sq[KS + r:KS + r + 1, :, :], mrow[:, r, :]).then_inc(m_stacked.sem, 16)
                sp.wait_ge(f_done.sem, f_done.at(b, 4))
                sp.dma_start(out[b].rearrange("(t p) d -> p t d", p=P), res_s[:, :, :]).then_inc(x_stored.sem, 16)
            sp.wait_ge(x_stored.sem, 16 * (NB + 1))

        @block.tensor
        def _(pe):
            mm = nc.tensor.matmul

            pe.wait_ge(w_in, 16 * N_LOADS)
            pe.wait_ge(pool_const, 1)
            pe.wait_ge(dve_const, 1)
            for _n in range(2):
                pe.sem_inc(pv_ready.sem, 1)
                pe.sem_inc(y_ready.sem, 1)

            def attn_project(b):
                pe.wait_ge(xn_done.sem, xn_done.at(b, 1))
                for c in range(C):
                    turn(xn, bank[c], c).then_inc(xn_turned.sem, 1)
                pe.wait_ge(xnt_done.sem, xnt_done.at(b, C))
                for g in range(2 * C):
                    for c in range(C):
                        last = mm(bank[2 + g][:, :], wqk[:, c, g * P:(g + 1) * P], xt[:, c, :],
                                  start=(c == 0), stop=(c == C - 1))
                    last.then_inc(qk_ready.sem, 1)
                for j in range(2):
                    for tb in (2 * j, 2 * j + 1):
                        o = (tb % 2) * D
                        for c in range(C):
                            last = mm(bank[6 + j][:, o:o + D], xt[:, c, tb * P:(tb + 1) * P], wv[:, c, :],
                                      start=(c == 0), stop=(c == C - 1))
                    last.then_inc(v_ready.sem, 1)

            def max_block(dst, h, qb, o):
                n = (qb + 1) * P
                mm(dst[:, o:o + n], sq[0:KS, h, qb * P:(qb + 1) * P], sk[0:KS, h, 0:n], start=True, stop=False)
                return mm(dst[:, o + n - P:o + n], ident_bf[:, :], mask_qk[:, :], start=False, stop=True)

            def max_pair(b, j):
                for un in range(UN):
                    g = UN * j + un
                    pe.wait_ge(mx_used.sem, mx_used.at(b, g - 1))
                    dst = bank[2 + g % 2]
                    h = 2 * j + un // 2
                    if un == 4:
                        max_block(dst, 2 * j, 1, 0)
                        last = max_block(dst, 2 * j + 1, 1, 2 * P)
                    elif un % 2 == 0:
                        last = max_block(dst, h, 3, 0)
                    else:
                        max_block(dst, h, 2, 0)
                        last = max_block(dst, h, 0, 3 * P)
                    last.then_inc(mx_ready.sem, 1)

            def max_rows(b):
                pe.wait_ge(negm_done.sem, negm_done.at(b, 1))
                pe.wait_ge(mx_used.sem, mx_used.at(b, HP * UN - 1))
                for qb in range(TB):
                    last = nc.tensor.transpose(bank[2][0:H, qb * P:(qb + 1) * P], negm[:, qb, :], ident[:, :])
                last.then_inc(mx_ready.sem, 1)

            def score_block(dst, h, kb, o):
                n = T - kb * P
                mm(dst[:, o:o + n], sk[:, h, kb * P:(kb + 1) * P], sq[:, h, kb * P:T], start=True, stop=False)
                return mm(dst[:, o:o + P], ident_bf[:, :], mask_kq[:, :], start=False, stop=True)

            def score_unit(b, g):
                j, un = divmod(g, UN)
                pe.wait_ge(exp_done.sem, exp_done.at(b, g - 1))
                dst = bank[g % 2]
                h = 2 * j + un // 2
                if un == 4:
                    score_block(dst, 2 * j, 2, 0)
                    last = score_block(dst, 2 * j + 1, 2, 2 * P)
                elif un % 2 == 0:
                    last = score_block(dst, h, 0, 0)
                else:
                    score_block(dst, h, 1, 0)
                    last = score_block(dst, h, 3, 3 * P)
                last.then_inc(st_ready.sem, 1)

            def value_part(b, j, hh, qb):
                for kb in range(qb + 1):
                    un, o = {0: (2 * hh, qb * P), 1: (2 * hh + 1, (qb - 1) * P),
                             2: (4, hh * 2 * P + (qb - 2) * P), 3: (2 * hh + 1, 3 * P)}[kb]
                    o2 = (hh * TB + qb) * (HD + 1)
                    last = mm(bank[4][:, o2:o2 + HD + 1], pt_v[:, j % 2, un, o:o + P], v_sb[:, kb, 2 * j + hh, :],
                              start=(kb == 0), stop=(kb == qb))
                return last

            def values(b, j):
                pe.wait_ge(exp_done.sem, exp_done.at(b, UN * (j + 1)))
                pe.wait_ge(pv_used.sem, pv_used.at(b, j))
                for hh in range(2):
                    for qb in range(TB):
                        last = value_part(b, j, hh, qb)
                last.then_inc(pv_ready.sem, 1)

            def attn_out(b):
                pe.wait_ge(pv_used.sem, pv_used.at(b, HP))
                pe.wait_ge(exp_done.sem, exp_done.at(b, HP * UN))
                for c in range(C):
                    turn(ao, bank[c], c).then_inc(ao_turned.sem, 1)
                pe.wait_ge(aot_done.sem, aot_done.at(b, C))
                pe.wait_ge(mx_used.sem, mx_used.at(b, HP * UN + 2))
                for j in range(2):
                    for tb in (2 * j, 2 * j + 1):
                        o = (tb % 2) * D
                        for c in range(C):
                            last = mm(bank[2 + j][:, o:o + D], xt[:, c, tb * P:(tb + 1) * P], wo[:, c, :],
                                      start=(c == 0), stop=(c == C - 1))
                    last.then_inc(wo_ready.sem, 1)

            def ffn(b, f):
                pe.wait_ge(xhat_f.sem, xhat_f.at(b, f + 1))
                for c in range(C):
                    turn(tok, bank[c], c).then_inc(f_turned.sem, 1)
                pe.wait_ge(ft_done.sem, ft_done.at(b, C * (f + 1)))
                for tb in range(TB):
                    for c in range(C):
                        last = mm(bank[4][:, tb * LR:(tb + 1) * LR], xt[:, c, tb * P:(tb + 1) * P], wdown[:, c, :],
                                  start=(c == 0), stop=(c == C - 1))
                last.then_inc(low_ready.sem, 1)
                if f == 0:
                    pe.wait_ge(x1_done.sem, x1_done.at(b, 2))
                else:
                    pe.wait_ge(x3_done.sem, x3_done.at(b, 2))
                for c in range(C):
                    for tb in range(TB):
                        o = (tb % 2) * D
                        mm(bank[2 + tb // 2][:, o:o + D], xt[:, c, tb * P:(tb + 1) * P], wbase[:, c, :],
                           start=(c == 0 and tb % 2 == 0), stop=False, skip_group_check=True)
                pe.wait_ge(hw_done.sem, hw_done.at(b, f + 1))
                for tb in range(TB):
                    last = nc.tensor.transpose(bank[5][0:(E + 1) * R, tb * P:(tb + 1) * P], hw[:, tb, :], ident[:, :])
                last.then_inc(hw_turned.sem, 1)
                pe.wait_ge(hwt_done.sem, hwt_done.at(b, f + 1))
                for tb in range(TB):
                    o = (tb % 2) * D
                    last = mm(bank[2 + tb // 2][:, o:o + D], hw_t[:, tb * P:(tb + 1) * P], wup[:, :],
                              start=False, stop=True, skip_group_check=True)
                    if tb % 2:
                        last.then_inc(f_ready.sem, 1)

            def ssm_project(b):
                pe.wait_ge(xhat_s.sem, xhat_s.at(b, 1))
                for c in range(C):
                    turn(tok, bank[c], c).then_inc(s_turned.sem, 1)
                pe.wait_ge(xst_done.sem, xst_done.at(b, C))
                for g in range(C):
                    for c in range(C):
                        last = mm(bank[2 + g][:, :], wg[:, c, g * P:(g + 1) * P], xs_t[:, c, TAPS - 1:],
                                  start=(c == 0), stop=(c == C - 1))
                    last.then_inc(g_ready.sem, 1)
                pe.wait_ge(xc_done.sem, xc_done.at(b, C))
                for c in range(C):
                    last = mm(bank[4][0:6 * NS, :], wbc[:, c, :, :], xc[:, c, :], start=(c == 0), stop=(c == C - 1))
                last.then_inc(bc_ready.sem, 1)
                for g in range(C):
                    for c in range(C):
                        last = mm(bank[6 + g][:, :], wd[:, c, g * P:(g + 1) * P], xc[:, c, :],
                                  start=(c == 0), stop=(c == C - 1))
                    last.then_inc(d_ready.sem, 1)
                pe.wait_ge(bc_done.sem, bc_done.at(b, 1))
                for n in range(NS):
                    pe.wait_ge(b_done.sem, b_done.at(b, n - 1))
                    mm(bank[n % 2][:, :], onehot[:, n, :], bcs[:, :], start=True, stop=True).then_inc(b_ready.sem, 1)

            def spread_c(b, n):
                pe.wait_ge(hc_done.sem, hc_done.at(b, n))
                mm(bank[5][:, :], onehot[:, NS + n, :], bcs[:, :], start=True, stop=True).then_inc(c_ready.sem, 1)

            def sum_states(b, n):
                pe.wait_ge(hc_done.sem, hc_done.at(b, n + 1))
                for tb in range(TB):
                    for c in range(C):
                        o = (tb % 2) * D + c * P
                        last = mm(bank[6 + tb // 2][:, o:o + P], hc[:, n % 2, c, tb * P:(tb + 1) * P], ident[:, :],
                                  start=(n == 0 and tb % 2 == 0 and c == 0), stop=(n == NS - 1),
                                  is_transpose=True, skip_group_check=True)
                last.then_inc(y_ready.sem, 1)

            def ssm_out(b):
                pe.wait_ge(y_done.sem, y_done.at(b, 2))
                pe.wait_ge(b_done.sem, b_done.at(b, NS))
                for c in range(C):
                    turn(tok, bank[c], c).then_inc(y_turned.sem, 1)
                pe.wait_ge(yg_done.sem, yg_done.at(b, C))
                for j in range(2):
                    for tb in (2 * j, 2 * j + 1):
                        o = (tb % 2) * D
                        for c in range(C):
                            last = mm(bank[2 + j][:, o:o + D], gate[:, c, tb * P:(tb + 1) * P], wso[:, c, :],
                                      start=(c == 0), stop=(c == C - 1))
                    last.then_inc(so_ready.sem, 1)

            with pe.Fori(0, NB) as b:
                attn_project(b)
                pe.wait_ge(stacked.sem, stacked.at(b, 2 * len(TERMS)))
                for j in range(HP):
                    max_pair(b, j)
                max_rows(b)
                pe.wait_ge(m_stacked.sem, m_stacked.at(b, 2))
                for un in range(UN):
                    score_unit(b, un)
                for j in range(HP):
                    if j + 1 < HP:
                        for un in range(UN):
                            score_unit(b, UN * (j + 1) + un)
                    values(b, j)
                attn_out(b)
                ffn(b, 0)
                ssm_project(b)
                spread_c(b, 0)
                for n in range(NS):
                    sum_states(b, n)
                    if n + 1 < NS:
                        spread_c(b, n + 1)
                ssm_out(b)
                ffn(b, 1)

        @block.scalar
        def _(act):
            A = nc.scalar.activation
            act.wait_ge(w_in, 16 * N_LOADS)
            A(a_neg[:, :, :], a_neg[:, :, :], ACT.Exp).then_inc(act_const, 1)
            act.wait_ge(dve_const, 1)
            for _n in range(2):
                act.sem_inc(exp_done.sem, 1)
                act.sem_inc(b_done.sem, 1)

            def copies(b, ready, done, dst, first=0):
                for c in range(C):
                    act.wait_ge(ready.sem, ready.at(b, first + c + 1))
                    nc.scalar.copy(dst[:, c, :], bank[c][:, :]).then_inc(done.sem, 1)

            def attn_project(b):
                copies(b, xn_turned, xnt_done, xt)
                for g in range(2 * C):
                    act.wait_ge(qk_ready.sem, qk_ready.at(b, g + 1))
                    A(qkf[:, g, :], bank[2 + g][:, :], ACT.Identity, bias=bqk[:, g:g + 1],
                                    scale=HD ** -0.5 if g < C else 1.0).then_inc(qk_biased.sem, 1)

            def exps(b, g):
                j, un = divmod(g, UN)
                if un == 0:
                    act.wait_ge(pv_ready.sem, pv_ready.at(b, j - 1))
                act.wait_ge(st_ready.sem, st_ready.at(b, g + 1))
                A(pt_v[:, j % 2, un, :], bank[g % 2][:, :], ACT.Exp).then_inc(exp_done.sem, 1)

            def attn_out(b):
                copies(b, ao_turned, aot_done, xt)

            def ffn(b, f):
                copies(b, f_turned, ft_done, xt, first=C * f)
                act.wait_ge(lg_done.sem, lg_done.at(b, f + 1))
                A(ex[:, :, :], lg[:, :, :], ACT.Exp).then_inc(ex_done.sem, 1)
                act.wait_ge(hw_turned.sem, hw_turned.at(b, f + 1))
                nc.scalar.copy(hw_t, bank[5][0:(E + 1) * R, :]).then_inc(hwt_done.sem, 1)

            def ssm_project(b):
                copies(b, s_turned, xst_done, xs_t[:, :, TAPS - 1:])
                for c in range(C):
                    act.wait_ge(conv_done.sem, conv_done.at(b, c + 1))
                    A(sp_t[:, c, :], xc[:, c, :], ACT.Tanh).then_inc(tanh_done.sem, 1)
                for c in range(C):
                    act.wait_ge(g_ready.sem, g_ready.at(b, c + 1))
                    A(gate[:, c, :], bank[2 + c][:, :], ACT.Tanh, bias=bg_c[:, c:c + 1], scale=0.5).then_inc(g_done.sem, 1)
                act.wait_ge(bc_ready.sem, bc_ready.at(b, 1))
                nc.scalar.copy(bcs[:, :], bank[4][0:6 * NS, :]).then_inc(bc_high.sem, 1)
                for c in range(C):
                    act.wait_ge(d_ready.sem, d_ready.at(b, c + 1))
                    A(dt[:, c, :], bank[6 + c][:, :], ACT.Relu, bias=bd_c[:, c:c + 1])
                    last = A(sp_t[:, c, :], bank[6 + c][:, :], ACT.Abs, bias=bd_c[:, c:c + 1])
                last.then_inc(act_s.sem, 1)
                act.wait_ge(act_s.sem, act_s.next(b))
                A(sp_t[:, :, :], sp_t[:, :, :], ACT.Exp, scale=-1.0).then_inc(act_s.sem, 1)
                act.wait_ge(act_s.sem, act_s.next(b))
                A(sp_t[:, :, :], sp_t[:, :, :], ACT.Ln, bias=1.0).then_inc(sp_done.sem, 1)
                for n in range(NS):
                    act.wait_ge(b_ready.sem, b_ready.at(b, n + 1))
                    nc.scalar.copy(b_all[:, n, :], bank[n % 2][:, :]).then_inc(b_done.sem, 1)

            def decays(b, n):
                if n == 0:
                    act.wait_ge(u_done.sem, u_done.at(b, 1))
                act.wait_ge(scan_done.sem, scan_done.at(b, n - 1))
                for c in range(C):
                    last = A(dec[:, n % 2, c, 1:T], dt[:, c, 1:T], ACT.Exp, scale=a_neg[:, c, n:n + 1])
                last.then_inc(dec_ready.sem, 1)

            def ssm_out(b):
                act.wait_ge(y_ready.sem, y_ready.at(b, NS))
                for j in range(2):
                    nc.scalar.copy(tok[:, 2 * j:2 * j + 2, :].rearrange("p t d -> p (t d)"), bank[6 + j][:, :]).then_inc(y_done.sem, 1)

            with act.Fori(0, NB) as b:
                attn_project(b)
                for g in range(HP * UN):
                    exps(b, g)
                attn_out(b)
                ffn(b, 0)
                ssm_project(b)
                for n in range(NS):
                    decays(b, n)
                ssm_out(b)
                ffn(b, 1)

        @block.vector
        def _(dve):
            V = nc.vector
            V.memset(dec[:, :, :, :], 0.0)
            V.memset(xs_t[:, :, 0:TAPS - 1], 0.0)
            V.memset(v_sb[:, :, :, HD:HD + 1], 1.0)
            V.memset(sk[KS:KS + 2, :, :], 1.0)
            V.memset(wts[:, :, :], 1.0)
            V.memset(half[:, :], -0.5)
            dve.wait_ge(w_in, 16 * N_LOADS)
            dve.wait_ge(act_const, 1)
            dve.wait_ge(pool_const, 1)
            V.tensor_scalar(a_neg[:, :, :], a_neg[:, :, :], -1.0, None, ALU.mult)
            V.tensor_scalar(bqk[:, 0:C], bqk[:, 0:C], HD ** -0.5, None, ALU.mult)
            V.tensor_scalar(bg_c[:, :], bg_c[:, :], 0.5, None, ALU.mult)
            V.tensor_scalar(cb[:, :], cb[:, :], 0.5, None, ALU.mult)
            V.tensor_scalar(cw[:, :, :], cw[:, :, :], 0.5, None, ALU.mult)
            V.tensor_copy(ident_bf[:, :], ident[:, :])
            V.tensor_scalar(wso[:, :, :], wso[:, :, :], 0.5, None, ALU.mult).then_inc(dve_const_step, 1)
            dve.wait_ge(dve_const_step, 1)
            dve.sem_inc(dve_const, 1)
            for t in (mx_used, scan_done):
                dve.sem_inc(t.sem, 1)
                dve.sem_inc(t.sem, 1)
            dve.sem_inc(pv_used.sem, 1)
            dve.sem_inc(hc_done.sem, 1)

            def normalise(b, k, src, steps, var, rsq, done, dst, mul, add):
                for tb in range(TB):
                    last = V.bn_stats(st[:, tb, :], src[:, tb, :])
                last.then_inc(steps.sem, 1)
                dve.wait_ge(steps.sem, steps.next(b))
                dve.sem_inc(waited, 1)
                for tb in range(TB):
                    last = V.bn_aggr(mv[:, tb, :], st[:, tb, :])
                last.then_inc(steps.sem, 1)
                dve.wait_ge(steps.sem, steps.next(b))
                V.tensor_scalar(va[:, :], mv[:, :, 1], mul, add, ALU.mult, ALU.add).then_inc(var.sem, 1)
                dve.wait_ge(rsq.sem, rsq.at(b, k + 1))
                V.scalar_tensor_tensor(nm[:, :], mv[:, :, 0], -1.0, rs[:, :], ALU.mult, ALU.mult).then_inc(steps.sem, 1)
                dve.wait_ge(steps.sem, steps.next(b))
                for tb in range(TB):
                    last = V.tensor_scalar(dst[:, tb, :], src[:, tb, :], rs[:, tb:tb + 1], nm[:, tb:tb + 1],
                                           ALU.mult, ALU.add)
                last.then_inc(done.sem, 1)

            def attn_project(b):
                dve.wait_ge(x_loaded.sem, x_loaded.at(b, 1))
                e1, e2 = 1e-5, 1e-6
                normalise(b, 0, x_in, dve_a, var_a, rs_a, xhat_a, tok, 1.0 + e2, e1 * e2)
                for j in range(2):
                    dve.wait_ge(v_ready.sem, v_ready.at(b, j + 1))
                    V.tensor_tensor(
                        v_sb[:, 2 * j:2 * j + 2, :, 0:HD],
                        bank[6 + j][:, :].rearrange("p (t h i) -> p t h i", t=2, h=H),
                        rows(bv_row, 2).rearrange("p t (h i) -> p t h i", h=H), ALU.add).then_inc(v_done.sem, 1)

            def maxima(b, g):
                dve.wait_ge(mx_ready.sem, mx_ready.at(b, g + 1))
                src = bank[2 + g % 2][:, :].rearrange("p (k n) -> p k n", k=TB)
                V.tensor_reduce(mxp[:, g // UN, g % UN, :], src, AXX, ALU.max).then_inc(mx_used.sem, 1)

            def max_rows(b):
                dve.wait_ge(mx_used.sem, mx_used.at(b, HP * UN))

                def neg(qb, src):
                    dst = negm[:, qb, :].rearrange("p (j h) -> p j h", h=2)
                    return V.tensor_reduce(dst, src, AXX, ALU.max, negate=True)

                neg(3, mxp[:, :, 0:3:2, :])
                neg(2, mxp[:, :, 1:4:2, 0:3])
                neg(0, mxp[:, :, 1:4:2, 3:4])
                neg(1, mxp[:, :, 4, :].rearrange("p j (h k) -> p j h k", h=2)).then_inc(negm_done.sem, 1)
                dve.wait_ge(mx_ready.sem, mx_ready.at(b, HP * UN + 1))
                V.tensor_copy(mrow[:, 0, :], bank[2][0:H, :]).then_inc(dve_m.sem, 1)
                dve.wait_ge(dve_m.sem, dve_m.next(b))
                V.tensor_tensor(mrow[:, 1, :], bank[2][0:H, :], mrow[:, 0, :], ALU.subtract).then_inc(mrow_done.sem, 1)
                dve.wait_ge(mrow_done.sem, mrow_done.at(b, 1))
                dve.sem_inc(mx_used.sem, 2)

            def head_norm(b, j):
                dve.wait_ge(pv_ready.sem, pv_ready.at(b, j + 1))
                pv = bank[4][:, 0:2 * TB * (HD + 1)].rearrange("p (g i) -> p g i", i=HD + 1)
                V.reciprocal(rc[:, :], pv[:, :, HD]).then_inc(dve_h.sem, 1)
                dve.wait_ge(dve_h.sem, dve_h.next(b))
                for hh in range(2):
                    h = 2 * j + hh
                    last = V.tensor_tensor(ao[:, :, h * HD:(h + 1) * HD], pv[:, hh * TB:(hh + 1) * TB, 0:HD],
                                           rc[:, hh * TB:(hh + 1) * TB, None].to_broadcast([P, TB, HD]), ALU.mult)
                last.then_inc(pv_used.sem, 1)

            def add_out(b, ready, done, src, dst, first=0):
                for j in range(2):
                    dve.wait_ge(ready.sem, ready.at(b, first + j + 1))
                    V.tensor_tensor(dst[:, 2 * j:2 * j + 2, :],
                                             bank[2 + j][:, :].rearrange("p (t d) -> p t d", t=2),
                                             src[:, 2 * j:2 * j + 2, :], ALU.add).then_inc(done.sem, 1)

            def attn_out(b):
                dve.wait_ge(res_done.sem, res_done.at(b, 1))
                add_out(b, wo_ready, x1_done, res_a, res_a)
                dve.wait_ge(x1_done.sem, x1_done.at(b, 2))

            def ffn(b, f):
                src = res_a if f == 0 else res_s
                normalise(b, f, src, dve_f, var_f, rs_f, xhat_f, tok, 1.0, 1e-5)
                dve.wait_ge(low_ready.sem, low_ready.at(b, f + 1))
                low = bank[4][:, 0:TB * LR].rearrange("p (t l) -> p t l", t=TB)
                V.tensor_tensor(lg[:, :, :], low[:, :, LR - E:LR], rb_row[:, None, :].to_broadcast([P, TB, E]), ALU.add).then_inc(dve_f.sem, 1)
                dve.wait_ge(dve_f.sem, dve_f.next(b))
                V.tensor_reduce(red[:, 0, :], lg[:, :, :], AXX, ALU.max).then_inc(dve_f.sem, 1)
                dve.wait_ge(dve_f.sem, dve_f.next(b))
                V.tensor_tensor(lg[:, :, :], lg[:, :, :], red[:, 0, :, None].to_broadcast([P, TB, E]),
                                            ALU.subtract).then_inc(lg_done.sem, 1)
                dve.wait_ge(ex_done.sem, ex_done.at(b, f + 1))
                mine = ex[:, :, :, None].to_broadcast([P, TB, E, E])
                other = ex[:, :, None, :].to_broadcast([P, TB, E, E])
                V.tensor_tensor(cmp_a[:, :, :, :], other, mine, ALU.is_gt)
                V.tensor_reduce(red[:, 1, :], ex[:, :, :], AXX, ALU.add)
                V.tensor_tensor(cmp_b[:, :, :, :], other, mine, ALU.is_equal).then_inc(dve_f.sem, 1)
                dve.wait_ge(dve_f.sem, dve_f.next(b))
                V.tensor_tensor(cmp_b[:, :, :, :], cmp_b[:, :, :, :],
                                   below[:, None, :, :].to_broadcast([P, TB, E, E]), ALU.mult).then_inc(dve_f.sem, 1)
                dve.wait_ge(dve_f.sem, dve_f.next(b))
                V.tensor_tensor(cmp_a[:, :, :, :], cmp_a[:, :, :, :], cmp_b[:, :, :, :], ALU.add).then_inc(dve_f.sem, 1)
                dve.wait_ge(dve_f.sem, dve_f.next(b))
                V.tensor_reduce(rank[:, :, :], cmp_a[:, :, :, :], AXX, ALU.add).then_inc(dve_f.sem, 1)
                dve.wait_ge(dve_f.sem, dve_f.next(b))
                V.scalar_tensor_tensor(rank[:, :, :], rank[:, :, :], 1.5, ex[:, :, :], ALU.is_lt, ALU.mult).then_inc(dve_f.sem, 1)
                dve.wait_ge(dve_f.sem, dve_f.next(b))
                V.tensor_reduce(red[:, 2, :], rank[:, :, :], AXX, ALU.add).then_inc(dve_f.sem, 1)
                dve.wait_ge(dve_f.sem, dve_f.next(b))
                V.scalar_tensor_tensor(red[:, 3, :], red[:, 1, :], 1e-6, red[:, 2, :], ALU.mult, ALU.add).then_inc(dve_f.sem, 1)
                dve.wait_ge(dve_f.sem, dve_f.next(b))
                V.reciprocal(red[:, 3, :], red[:, 3, :]).then_inc(dve_f.sem, 1)
                dve.wait_ge(dve_f.sem, dve_f.next(b))
                V.tensor_tensor(wts[:, :, 1:], rank[:, :, :], red[:, 3, :, None].to_broadcast([P, TB, E]), ALU.mult).then_inc(dve_f.sem, 1)
                dve.wait_ge(dve_f.sem, dve_f.next(b))
                V.tensor_tensor(
                    hw.rearrange("p t (e r) -> p t e r", r=R),
                    low[:, :, 0:(E + 1) * R].rearrange("p t (e r) -> p t e r", r=R),
                    wts[:, :, :, None].to_broadcast([P, TB, E + 1, R]), ALU.mult).then_inc(hw_done.sem, 1)
                dve.wait_ge(bias_f.sem, bias_f.at(b, f + 1))
                if f == 0:
                    dve.wait_ge(x_stored.sem, x_stored.at(b, 0))
                add_out(b, f_ready, f_done, src, res_s, first=2 * f)
                dve.wait_ge(f_done.sem, f_done.at(b, 2 * f + 2))

            def ssm_project(b):
                normalise(b, 0, res_s, dve_s, var_s, rs_s, xhat_s, tok, 1.0, 1e-5)
                dve.wait_ge(xst_done.sem, xst_done.at(b, C))
                for k in range(TAPS):
                    for c in range(C):
                        if k == 0:
                            last = V.tensor_scalar(xc[:, c, :], xs_t[:, c, 0:T], cw[:, c, 0:1], cb[:, c:c + 1],
                                                   ALU.mult, ALU.add)
                        else:
                            last = V.scalar_tensor_tensor(xc[:, c, :], xs_t[:, c, k:k + T], cw[:, c, k:k + 1],
                                                          xc[:, c, :], ALU.mult, ALU.add)
                        if k == TAPS - 1:
                            last.then_inc(conv_done.sem, 1)
                    if k < TAPS - 1:
                        last.then_inc(dve_s.sem, 1)
                        dve.wait_ge(dve_s.sem, dve_s.next(b))
                for c in range(C):
                    dve.wait_ge(tanh_done.sem, tanh_done.at(b, c + 1))
                    V.scalar_tensor_tensor(xc[:, c, :], sp_t[:, c, :], 1.0, xc[:, c, :], ALU.add, ALU.mult).then_inc(xc_done.sem, 1)
                dve.wait_ge(bc_high.sem, bc_high.at(b, 1))
                V.tensor_tensor(bcr[:, :], bank[4][0:6 * NS, :], bcs[:, :], ALU.subtract).then_inc(dve_s.sem, 1)
                dve.wait_ge(dve_s.sem, dve_s.next(b))
                V.tensor_copy(bcs[2 * NS:4 * NS, :], bcr[2 * NS:4 * NS, :])
                V.tensor_copy(bcs[4 * NS:6 * NS, :], bcr[4 * NS:6 * NS, :]).then_inc(dve_s.sem, 1)
                dve.wait_ge(dve_s.sem, dve_s.next(b))
                V.tensor_tensor(bcs[4 * NS:6 * NS, :], bcr[4 * NS:6 * NS, :], bcs[4 * NS:6 * NS, :],
                                            ALU.subtract).then_inc(bc_done.sem, 1)

            def scan(b, n):
                dve.wait_ge(dec_ready.sem, dec_ready.at(b, n + 1))
                dve.wait_ge(inp_ready.sem, inp_ready.at(b, n + 1))
                dve.wait_ge(y_ready.sem, y_ready.at(b, n - 1))
                h, d, i = (t[:, n % 2, :, :].rearrange("p c t -> p (c t)") for t in (hc, dec, inp))
                V.tensor_tensor_scan(h, d, i, 0.0, ALU.mult, ALU.add).then_inc(scan_done.sem, 1)

            def times_c(b, n):
                dve.wait_ge(scan_done.sem, scan_done.at(b, n + 1))
                dve.wait_ge(c_ready.sem, c_ready.at(b, n + 1))
                V.tensor_tensor(hc[:, n % 2, :, :], hc[:, n % 2, :, :],
                                            bank[5][:, None, :].to_broadcast([P, C, T]), ALU.mult).then_inc(hc_done.sem, 1)

            def ssm_out(b):
                for c in range(C):
                    dve.wait_ge(y_turned.sem, y_turned.at(b, c + 1))
                    V.scalar_tensor_tensor(gate[:, c, :], gate[:, c, :], 1.0, bank[c][:, :],
                                                       ALU.add, ALU.mult).then_inc(yg_done.sem, 1)
                dve.wait_ge(bias_s.sem, bias_s.at(b, 1))
                add_out(b, so_ready, x3_done, res_s, res_s)
                dve.wait_ge(x3_done.sem, x3_done.at(b, 2))

            with dve.Fori(0, NB) as b:
                attn_project(b)
                for g in range(HP * UN):
                    maxima(b, g)
                max_rows(b)
                for j in range(HP):
                    head_norm(b, j)
                attn_out(b)
                ffn(b, 0)
                ssm_project(b)
                for n in range(NS):
                    scan(b, n)
                    times_c(b, n)
                ssm_out(b)
                ffn(b, 1)

        @block.gpsimd
        def _(pool):
            G = nc.gpsimd
            G.memset(ident[:, :], 0.0)
            G.memset(mask_qk[:, :], 0.0)
            G.memset(mask_kq[:, :], 0.0)
            G.memset(below[:, :, :], 1.0)
            G.memset(onehot[:, :, :], 0.0).then_inc(pool_const_step, 1)
            pool.wait_ge(pool_const_step, 1)
            G.affine_select(out=ident[:, :], in_=ident[:, :], compare_op=ALU.not_equal, fill=1.0, base=0,
                            pattern=[[-1, P]], channel_multiplier=1)
            G.affine_select(out=mask_qk[:, :], in_=mask_qk[:, :], compare_op=ALU.is_ge, fill=BIG, base=0,
                            pattern=[[-1, P]], channel_multiplier=1)
            G.affine_select(out=mask_kq[:, :], in_=mask_kq[:, :], compare_op=ALU.is_ge, fill=BIG, base=0,
                            pattern=[[1, P]], channel_multiplier=-1)
            G.affine_select(out=below[:, :, :], in_=below[:, :, :], compare_op=ALU.is_gt, fill=0.0, base=0,
                            pattern=[[1, E], [-1, E]], channel_multiplier=0)
            for j in range(3):
                G.affine_select(out=onehot[:, :, :], in_=onehot[:, :, :], compare_op=ALU.not_equal, fill=1.0,
                                base=-2 * NS * j, pattern=[[-1, 2 * NS], [0, P]],
                                channel_multiplier=1).then_inc(pool_const_step, 1)
                pool.wait_ge(pool_const_step, 2 + j)
            pool.sem_inc(pool_const, 1)
            pool.wait_ge(w_in, 16 * N_LOADS)
            pool.wait_ge(dve_const, 1)
            pool.sem_inc(x_used.sem, 1)

            def rsqrt(b, n, var, rsq):
                pool.wait_ge(var.sem, var.at(b, n + 1))
                G.tensor_tensor(rs[:, :], va[:, :], half[:, :], ALU.pow).then_inc(rsq.sem, 1)

            def attn_project(b):
                rsqrt(b, 0, var_a, rs_a)
                pool.wait_ge(xhat_a.sem, xhat_a.at(b, 1))
                G.tensor_tensor(xn[:, :, :], tok[:, :, :], rows(w_row), ALU.mult).then_inc(xn_done.sem, 1)
                pool.wait_ge(xn_done.sem, xn_done.at(b, 1))
                G.tensor_tensor(res_a[:, :, :], x_in[:, :, :], xn[:, :, :], ALU.add).then_inc(x_used.sem, 1)
                pool.wait_ge(x_used.sem, x_used.at(b, 1))
                G.tensor_tensor(res_a[:, :, :], res_a[:, :, :], rows(bo_row), ALU.add).then_inc(res_done.sem, 1)
                pool.wait_ge(qk_biased.sem, qk_biased.at(b, 2 * C))
                pool.sem_inc(waited, 1)
                G.tensor_copy(parts[:, 0, :, :], qkf).then_inc(part_done.sem, 1)
                pool.wait_ge(part_done.sem, part_done.at(b, 1))
                G.tensor_tensor(qkf, qkf, parts[:, 0, :, :], ALU.subtract).then_inc(pool_a.sem, 1)
                pool.wait_ge(pool_a.sem, pool_a.next(b))
                pool.sem_inc(waited, 1)
                G.tensor_copy(parts[:, 1, :, :], qkf).then_inc(part_done.sem, 1)
                pool.wait_ge(part_done.sem, part_done.at(b, 2))
                G.tensor_tensor(parts[:, 2, :, :], qkf, parts[:, 1, :, :], ALU.subtract).then_inc(part_done.sem, 1)

            def ffn(b, f):
                src = res_a if f == 0 else res_s
                rsqrt(b, f, var_f, rs_f)
                pool.wait_ge(xhat_f.sem, xhat_f.at(b, f + 1))
                G.tensor_tensor(src[:, :, :], src[:, :, :], rows(bb_row), ALU.add).then_inc(bias_f.sem, 1)

            def ssm_project(b):
                rsqrt(b, 0, var_s, rs_s)
                pool.wait_ge(xhat_s.sem, xhat_s.at(b, 1))
                G.tensor_tensor(res_s[:, :, :], res_s[:, :, :], rows(bso_row), ALU.add).then_inc(bias_s.sem, 1)
                pool.wait_ge(sp_done.sem, sp_done.at(b, 1))
                G.tensor_tensor(dt[:, :, :], dt[:, :, :], sp_t[:, :, :], ALU.add).then_inc(u_done.sem, 1)
                pool.wait_ge(u_done.sem, u_done.at(b, 1))
                G.tensor_tensor(u[:, :, :], dt[:, :, :], xc[:, :, :], ALU.mult).then_inc(u_done.sem, 1)
                pool.wait_ge(u_done.sem, u_done.at(b, 2))

            def inputs(b, n):
                pool.wait_ge(b_done.sem, b_done.at(b, n + 1))
                pool.wait_ge(scan_done.sem, scan_done.at(b, n - 1))
                G.tensor_tensor(inp[:, n % 2, :, :], u[:, :, :],
                                              b_all[:, n:n + 1, :].to_broadcast([P, C, T]), ALU.mult).then_inc(inp_ready.sem, 1)

            with pool.Fori(0, NB) as b:
                attn_project(b)
                ffn(b, 0)
                ssm_project(b)
                for n in range(NS):
                    inputs(b, n)
                ffn(b, 1)


        assert all(t.n % t.per == 0 for t in tallies)


def kernel(**inputs):
    import numpy as np
    import concourse.bacc as bacc
    from concourse.bass_utils import run_bass_kernel_spmd

    g = {k: np.asarray(v) for k, v in inputs.items()}
    a, s, f = "L0_attn_a_", "L0_attn_b_", "L0_ffn_"
    E, R, D = g[f + "routed_A"].shape
    t = np.transpose

    def by_partition(*vectors):
        return t(np.concatenate(vectors).reshape(-1, P))

    arrays = {
        "x": g[a + "x"], "norm_w": g[a + "norm_w"],
        "wqk_t": np.concatenate([t(g[a + "Wq"]), t(g[a + "Wk"])], 1), "bqk": by_partition(g[a + "bq"], g[a + "bk"]),
        "wv_t": t(g[a + "Wv"]), "bv": g[a + "bv"], "wo_t": t(g[a + "Wo"]), "bo": g[a + "bo"],
        "conv_w": g[s + "conv_w"][:, 0, :], "conv_b": by_partition(g[s + "conv_b"]), "wd_t": t(g[s + "Wd"]), "bd": by_partition(g[s + "bd"]),
        "wbc_t": np.concatenate([t(g[s + "Wb"]), t(g[s + "Wc"])], 1), "log_a": g[s + "log_a"],
        "wg_t": t(g[s + "Wg"]), "bg": by_partition(g[s + "bg"]), "wso_t": t(g[s + "Wo"]), "bso": g[s + "bo"],
        "base_t": t(g[f + "base_W"]), "base_b": g[f + "base_b"],
        "down_t": np.concatenate([t(g[f + "shared_A"]), t(g[f + "routed_A"].reshape(E * R, D)), t(g[f + "router_W"])], 1),
        "up_s": np.concatenate([t(g[f + "shared_B"]), t(g[f + "routed_B"], (0, 2, 1)).reshape(E * R, D)], 0),
        "router_b": g[f + "router_b"],
    }
    arrays = {f"in_{k}": np.ascontiguousarray(v) for k, v in arrays.items()}
    nc = bacc.Bacc("TRN2", target_bir_lowering=False, num_devices=1)
    args = [nc.dram_tensor(k, v.shape, mybir.dt.from_np(v.dtype), kind="ExternalInput").ap() for k, v in arrays.items()]
    out = nc.dram_tensor("out", g[a + "x"].shape, F32, kind="ExternalOutput").ap()
    hybrid_block(nc, *args, out)
    r = run_bass_kernel_spmd(nc, [arrays], core_ids=[0])
    return r.results[0]["out"]
```

```python
from contextlib import ExitStack

import concourse.bass as bass
from concourse import mybir

F32 = mybir.dt.float32
BF16 = mybir.dt.bfloat16
ALU = mybir.AluOpType
ACT = mybir.ActivationFunctionType
AXX = mybir.AxisListType.X

P = 128
BIG = -1.0e30


class Tally:

    def __init__(self, sem, per, credit=0, step=1):
        self.sem, self.per, self.credit, self.step = sem, per, credit, step
        self.n = 0

    def at(self, b, n):
        return b * (self.per * self.step) + (n * self.step + self.credit)

    def next(self, b):
        self.n += 1
        return self.at(b, (self.n - 1) % self.per + 1)


def hybrid_block(nc, x, norm_w, wqk_t, bqk_c, wv_t, bv, wo_t, bo, conv_w, conv_b, wd_t, bd, wbc_t,
                 log_a, wg_t, bg, wso_t, bso, base_t, base_b, down_t, up_s, router_b, out):
    NB, T, D = x.shape
    C = D // P
    TB = T // P
    H = 16
    HD = D // H
    NS = log_a.shape[1]
    E = router_b.shape[0]
    R = up_s.shape[0] // (E + 1)
    LR = down_t.shape[1]
    HP = H // 2
    UN = 5
    TAPS = conv_w.shape[1]
    RB = 8
    TERMS = [(0, 0), (0, 1), (1, 0), (0, 2), (2, 0), (1, 1)]
    KS = len(TERMS) * HD

    ctx = ExitStack()
    with ctx:
        def sb(name, shape, dt=F32):
            return ctx.enter_context(nc.sbuf_tensor(name, shape, dt))

        def sem(name):
            return ctx.enter_context(nc.semaphore(name))

        def tally(name, per, credit=0, step=1):
            t = Tally(sem(name), per, credit, step)
            tallies.append(t)
            return t

        tallies = []
        bank = [ctx.enter_context(nc.psum_tensor(f"bank{i}", [P, 512], F32)) for i in range(8)]

        ident = sb("ident", [P, P])
        ident_bf = sb("ident_bf", [P, P], BF16)
        mask_qk = sb("mask_qk", [P, P], BF16)
        mask_kq = sb("mask_kq", [P, P], BF16)
        onehot = sb("onehot", [3 * 2 * NS, 2 * NS, P], BF16)
        wqk = sb("wqk", [P, C, 2 * D])
        wv = sb("wv", [P, C, D])
        wo = sb("wo", [P, C, D])
        wd = sb("wd", [P, C, D])
        wg = sb("wg", [P, C, D])
        wso = sb("wso", [P, C, D])
        wbase = sb("wbase", [P, C, D])
        wdown = sb("wdown", [P, C, LR])
        wup = sb("wup", [(E + 1) * R, D])
        wbc = sb("wbc", [P, C, 3, 2 * NS])
        bqk = sb("bqk", [P, 2 * C])
        bd_c = sb("bd_c", [P, C])
        bg_c = sb("bg_c", [P, C])
        cw = sb("cw", [P, C, TAPS])
        cb = sb("cb", [P, C])
        a_neg = sb("a_neg", [P, C, NS])
        w_row = sb("w_row", [P, D])
        bv_row = sb("bv_row", [P, D])
        bo_row = sb("bo_row", [P, D])
        bso_row = sb("bso_row", [P, D])
        bb_row = sb("bb_row", [P, D])
        rb_row = sb("rb_row", [P, E])
        below = sb("below", [P, E, E])
        half = sb("half", [P, TB])

        x_in = sb("x_in", [P, TB, D])
        res_a = sb("res_a", [P, TB, D])
        res_s = sb("res_s", [P, TB, D])
        tok = sb("tok", [P, TB, D])
        xn = sb("xn", [P, TB, D])
        ao = sb("ao", [P, TB, D])
        y_tok = sb("y_tok", [P, TB, D])
        x_out = sb("x_out", [P, TB, D])
        xt_a = sb("xt_a", [P, C, T])
        xt_b = sb("xt_b", [P, C, T])
        pt = sb("pt", [P, 2 * UN * 512])
        pt_v = pt[:, :].rearrange("p (r u n) -> p r u n", r=2, u=UN)
        qkf = pt[:, 0:2 * C * T].rearrange("p (g t) -> p g t", g=2 * C)
        parts = pt[:, 2 * C * T:5 * C * T].bitcast(BF16).rearrange("p (j g t) -> p j g t", j=3, g=2 * C)
        sq = sb("sq", [KS + 2, H, T], BF16)
        sk = sb("sk", [KS + 2, H, T], BF16)
        v_sb = sb("v_sb", [P, TB, H, HD + 1])
        mxp = sb("mxp", [P, HP, UN, TB])
        negm = sb("negm", [P, TB, H])
        mrow = sb("mrow", [H, 2, T], BF16)
        rc = sb("rc", [P, 2 * TB])
        st = sb("st", [P, TB, 6])
        mv = sb("mv", [P, TB, 2])
        va = sb("va", [P, TB])
        rs = sb("rs", [P, TB])
        nm = sb("nm", [P, TB])
        lg = sb("lg", [P, TB, E])
        ex = sb("ex", [P, TB, E])
        cmp_a = sb("cmp_a", [P, TB, E, E])
        cmp_b = sb("cmp_b", [P, TB, E, E])
        rank = sb("rank", [P, TB, E])
        red = sb("red", [P, 4, TB])
        wts = sb("wts", [P, TB, E + 1])
        xs_t = sb("xs_t", [P, C, TAPS - 1 + T])
        xc = sb("xc", [P, C, T])
        sp_t = sb("sp_t", [P, C, T])
        hw = sp_t[:, 0, 0:TB * (E + 1) * R].rearrange("p (t f) -> p t f", t=TB)
        hw_t = sp_t[0:(E + 1) * R, 1, :]
        dt = sb("dt", [P, C, T])
        u = sb("u", [P, C, T])
        gate = sb("gate", [P, C, T])
        bcs = sb("bcs", [3 * 2 * NS, T], BF16)
        bcr = sb("bcr", [3 * 2 * NS, T])
        b_all = sb("b_all", [P, RB, T])
        dec = sb("dec", [P, 2, C, T])
        inp = sb("inp", [P, 2, C, T])
        hc = sb("hc", [P, 2, C, T])

        scratch = nc.dram_tensor("qk_parts", [NB, 3, 2 * C, P, T], BF16, kind="Internal").ap()

        FFN = ((tok, xt_a, 0, 2, 3, 5), (y_tok, xt_b, 6, 0, 3, 1))

        w_in = sem("weights_loaded")
        pool_const = sem("pool_constants")
        dve_const = sem("dve_constants")
        act_const = sem("act_constants")
        dve_const_step = sem("dve_constant_step")
        pool_const_step = sem("pool_constant_steps")
        waited = sem("waited")

        x_loaded = tally("x_loaded", 1, step=16)
        x_used = tally("x_used", 1, credit=1)
        var_a, rs_a = tally("attn_variance", 1), tally("attn_rsqrt", 1)
        xhat_a = tally("attn_normalised", 1)
        xn_done = tally("xn_done", 1)
        res_done = tally("res_done", 1)
        xn_turned = tally("xn_turned", C)
        xnt_done = tally("xnt_done", C)
        qk_ready = tally("qk_ready", 2 * C)
        qk_biased = tally("qk_biased", 2 * C)
        v_ready = tally("v_ready", 2)
        v_done = tally("v_done", 2)
        high_off = tally("high_parts_off", 2)
        mid_done = tally("middle_parts", 2)
        low_done = tally("low_parts", 2)
        part_stored = tally("part_stored", 3, step=16)
        stacked = tally("stacked", 2 * len(TERMS), step=16)
        mx_ready = tally("scores_for_max", HP * UN + 1)
        mx_used = tally("scores_for_max_used", HP * UN + 2, credit=2)
        negm_done = tally("negm_done", 1)
        mrow_done = tally("mrow_done", 1)
        m_stacked = tally("max_stacked", 2, step=16)
        st_ready = tally("scores_ready", HP * UN)
        exp_done = tally("exp_done", HP * UN, credit=2)
        pv_ready = tally("pv_ready", HP, credit=2)
        pv_used = tally("pv_used", HP, credit=1)
        ao_turned = tally("ao_turned", C)
        aot_done = tally("aot_done", C)
        wo_ready = tally("wo_ready", 2)
        x1_done = tally("x1_done", 2)
        var_f, rs_f, xhat_f, bias_f, f_turned, ft_done, low_ready, lg_done, ex_done, hw_done, hw_turned, hwt_done, f_ready, f_done = (
            [tally(f"ffn{f}_{name}", per) for f in range(2)] for name, per in
            (("variance", 1), ("rsqrt", 1), ("normalised", 1), ("bias_added", 1), ("turned", C), ("turned_copied", C),
             ("low_rank", 1), ("logits", 1), ("exp", 1), ("weighted", 1), ("weighted_turned", 1), ("weighted_copied", 1),
             ("ready", 2), ("done", 2)))
        x_stored = tally("x_stored", 1, credit=16, step=16)
        var_s, rs_s = tally("ssm_variance", 1), tally("ssm_rsqrt", 1)
        xhat_s = tally("ssm_normalised", 1)
        bias_s = tally("ssm_bias_added", 1)
        s_turned = tally("ssm_turned", C)
        xst_done = tally("xst_done", C)
        conv_done = tally("conv_done", C)
        tanh_done = tally("tanh_done", C)
        xc_done = tally("xc_done", C)
        g_ready = tally("gate_ready", C)
        g_done = tally("gate_done", C)
        d_ready = tally("delta_ready", C)
        sp_done = tally("softplus_parts", 1)
        u_done = tally("u_done", 2)
        bc_ready = tally("bc_ready", 1)
        bc_high = tally("bc_high", 1)
        bc_done = tally("bc_done", 1)
        b_ready = tally("b_spread", NS)
        b_done = tally("b_copied", NS, credit=2)
        dec_ready = tally("decay_ready", NS)
        inp_ready = tally("input_ready", NS)
        scan_done = tally("scan_done", NS, credit=2)
        c_ready = tally("c_spread", NS)
        hc_done = tally("hc_done", NS, credit=1)
        y_ready = tally("y_summed", NS, credit=2)
        y_done = tally("y_copied", 2)
        y_turned = tally("y_turned", C)
        yg_done = tally("gated_y", C)
        so_ready = tally("ssm_out_ready", 2)
        x3_done = tally("x3_done", 2)
        dve_a = tally("dve_attn_steps", 3)
        dve_m = tally("dve_max_steps", 1)
        dve_h = tally("dve_head_steps", HP)
        dve_n = [tally(f"dve_normalise_steps{k}", 3) for k in range(3)]
        dve_r = [tally(f"dve_router_steps{f}", 11) for f in range(2)]
        dve_s = tally("dve_ssm_steps", TAPS - 1 + 2)
        act_s = tally("act_ssm_steps", 2)

        block = ctx.enter_context(nc.Block())

        def rows(t, n=TB):
            return t[:, None, :].to_broadcast([P, n, D])

        MSLOTS = 5
        MU = HP * UN // MSLOTS
        HSLOT = MSLOTS + 2
        LN_SLOT = NS - 3
        B_FIRST = 4
        B_SLOT = {0: (4, 5), 1: (6, 7), 2: (8, 9), 3: (10,), 4: (11, 12), 5: (13,), 6: (14, 15)}
        N_LOADS = 24

        @block.sync
        def _(sp):
            def chunked(w):
                return w.rearrange("(c p) n -> p c n", p=P)

            def load_x(b):
                sp.wait_ge(x_used.sem, x_used.at(b, 0))
                sp.dma_start(x_in[:, :, :], x[b].rearrange("(t p) d -> p t d", p=P)).then_inc(x_loaded.sem, 16)

            loads = [
                (w_row[:, :], norm_w[None, :].to_broadcast([P, D])),
                (wqk[:, :, :], chunked(wqk_t)), (bqk[:, :], bqk_c), (wv[:, :, :], chunked(wv_t)),
                (bv_row[:, :], bv[None, :].to_broadcast([P, D])), (bo_row[:, :], bo[None, :].to_broadcast([P, D])),
                (a_neg[:, :, :], chunked(log_a)), (bg_c[:, :], bg), (cw[:, :, :], chunked(conv_w)),
                (cb[:, :], conv_b), (wso[:, :, :], chunked(wso_t)), (wo[:, :, :], chunked(wo_t)),
                (wd[:, :, :], chunked(wd_t)), (wg[:, :, :], chunked(wg_t)),
                (wbase[:, :, :], chunked(base_t)), (wdown[:, :, :], chunked(down_t)), (wup[:, :], up_s),
                (bd_c[:, :], bd), (bso_row[:, :], bso[None, :].to_broadcast([P, D])),
                (bb_row[:, :], base_b[None, :].to_broadcast([P, D])),
                (rb_row[:, :], router_b[None, :].to_broadcast([P, E])),
            ]
            loads += [(wbc[:, :, j, :], chunked(wbc_t)) for j in range(3)]
            assert len(loads) == N_LOADS

            def max_rows(b):
                sp.wait_ge(mrow_done.sem, mrow_done.at(b, 1))
                for r in range(2):
                    sp.dma_start(sq[KS + r:KS + r + 1, :, :], mrow[:, r, :]).then_inc(m_stacked.sem, 16)

            def stack(b):
                for j, made in enumerate((qk_biased, mid_done, low_done)):
                    sp.wait_ge(made.sem, made.at(b, made.per))
                    sp.dma_start(scratch[b, j].rearrange("g p t -> p g t"),
                                 parts[:, j, :, :]).then_inc(part_stored.sem, 16)
                sp.wait_ge(part_stored.sem, part_stored.at(b, 3))
                for s, (jq, jk) in enumerate(TERMS):
                    for dst, j, g in ((sq, jq, 0), (sk, jk, C)):
                        src = scratch[b, j, g:g + C].rearrange("g (h i) t -> i (g h) t", i=HD)
                        sp.dma_start(dst[s * HD:(s + 1) * HD, :, :], src).then_inc(stacked.sem, 16)

            def store(b):
                sp.wait_ge(f_done[1].sem, f_done[1].at(b, 2))
                sp.dma_start(out[b].rearrange("(t p) d -> p t d", p=P), x_out[:, :, :]).then_inc(x_stored.sem, 16)

            load_x(0)
            for dst, src in loads:
                sp.dma_start(dst, src).then_inc(w_in, 16)
            sp.sem_inc(x_stored.sem, 16)
            stack(0)
            load_x(1)
            max_rows(0)
            stack(1)
            with sp.Fori(1, NB - 1) as i:
                load_x(i + 1)
                max_rows(i)
                stack(i + 1)
                store(i - 1)
            max_rows(NB - 1)
            store(NB - 2)
            store(NB - 1)
            sp.wait_ge(x_stored.sem, 16 * (NB + 1))

        @block.tensor
        def _(pe):
            mm = nc.tensor.matmul

            def turn(src, dst, c):
                for tb in range(TB):
                    last = nc.tensor.transpose(dst[:, tb * P:(tb + 1) * P], src[:, tb, c * P:(c + 1) * P],
                                               ident[:, :])
                return last

            def by_columns(dst, w, src, g):
                for c in range(C):
                    last = mm(dst, w[:, c, g * P:(g + 1) * P], src[:, c, :], start=(c == 0), stop=(c == C - 1))
                return last

            def by_tokens(dst, src, w, j):
                for tb in (2 * j, 2 * j + 1):
                    o = (tb % 2) * D
                    for c in range(C):
                        last = mm(dst[:, o:o + D], src[:, c, tb * P:(tb + 1) * P], w[:, c, :],
                                  start=(c == 0), stop=(c == C - 1))
                return last

            def turn_xn(b, first):
                pe.wait_ge(xn_done.sem, xn_done.at(b, 1))
                if not first:
                    pe.wait_ge(mx_used.sem, mx_used.at(b, 0))
                for c in range(C):
                    turn(xn, bank[2 + c], c).then_inc(xn_turned.sem, 1)

            def project_qkv(b, first):
                pe.wait_ge(xnt_done.sem, xnt_done.at(b, C))
                for g in range(2 * C):
                    by_columns(bank[g][:, :], wqk, xt_b, g).then_inc(qk_ready.sem, 1)
                for j in range(2):
                    by_tokens(bank[6 + j], xt_b, wv, j).then_inc(v_ready.sem, 1)

            def max_block(dst, h, qb, o):
                n = (qb + 1) * P
                mm(dst[:, o:o + n], sq[0:KS, h, qb * P:(qb + 1) * P], sk[0:KS, h, 0:n], start=True, stop=False)
                return mm(dst[:, o + n - P:o + n], ident_bf[:, :], mask_qk[:, :], start=False, stop=True)

            def max_unit(b, g):
                j, un = divmod(g, UN)
                if g == 0:
                    pe.wait_ge(stacked.sem, stacked.at(b, 2 * len(TERMS)))
                pe.wait_ge(mx_used.sem, mx_used.at(b, g - 1))
                dst = bank[2 + g % 2]
                h = 2 * j + un // 2
                if un == 4:
                    max_block(dst, 2 * j, 1, 0)
                    last = max_block(dst, 2 * j + 1, 1, 2 * P)
                elif un % 2 == 0:
                    last = max_block(dst, h, 3, 0)
                else:
                    max_block(dst, h, 2, 0)
                    last = max_block(dst, h, 0, 3 * P)
                last.then_inc(mx_ready.sem, 1)

            def max_rows(b):
                pe.wait_ge(negm_done.sem, negm_done.at(b, 1))
                for qb in range(TB):
                    last = nc.tensor.transpose(bank[2][0:H, qb * P:(qb + 1) * P], negm[:, qb, :], ident[:, :])
                last.then_inc(mx_ready.sem, 1)

            def score_block(dst, h, kb, o):
                n = T - kb * P
                mm(dst[:, o:o + n], sk[:, h, kb * P:(kb + 1) * P], sq[:, h, kb * P:T], start=True, stop=False)
                return mm(dst[:, o:o + P], ident_bf[:, :], mask_kq[:, :], start=False, stop=True)

            def score_unit(b, g):
                j, un = divmod(g, UN)
                if g == 0:
                    pe.wait_ge(m_stacked.sem, m_stacked.at(b, 2))
                pe.wait_ge(exp_done.sem, exp_done.at(b, g - 1))
                dst = bank[g % 2]
                h = 2 * j + un // 2
                if un == 4:
                    score_block(dst, 2 * j, 2, 0)
                    last = score_block(dst, 2 * j + 1, 2, 2 * P)
                elif un % 2 == 0:
                    last = score_block(dst, h, 0, 0)
                else:
                    score_block(dst, h, 1, 0)
                    last = score_block(dst, h, 3, 3 * P)
                last.then_inc(st_ready.sem, 1)

            def values(b, j):
                pe.wait_ge(exp_done.sem, exp_done.at(b, UN * (j + 1)))
                pe.wait_ge(pv_used.sem, pv_used.at(b, j))
                for hh in range(2):
                    for qb in range(TB):
                        for kb in range(qb + 1):
                            un, o = {0: (2 * hh, qb * P), 1: (2 * hh + 1, (qb - 1) * P),
                                     2: (4, hh * 2 * P + (qb - 2) * P), 3: (2 * hh + 1, 3 * P)}[kb]
                            o2 = (hh * TB + qb) * (HD + 1)
                            last = mm(bank[4][:, o2:o2 + HD + 1], pt_v[:, j % 2, un, o:o + P],
                                      v_sb[:, kb, 2 * j + hh, :], start=(kb == 0), stop=(kb == qb))
                last.then_inc(pv_ready.sem, 1)

            def turn_ao(b):
                pe.wait_ge(pv_used.sem, pv_used.at(b, HP))
                pe.wait_ge(exp_done.sem, exp_done.at(b, HP * UN))
                for c in range(C):
                    turn(ao, bank[c], c).then_inc(ao_turned.sem, 1)

            def attn_out(b):
                pe.wait_ge(aot_done.sem, aot_done.at(b, C))
                for j in range(2):
                    by_tokens(bank[4 + j], xt_a, wo, j).then_inc(wo_ready.sem, 1)

            def ffn_in(b, f):
                tokens, xt, t0, low, o0 = FFN[f][0:5]
                pe.wait_ge(xhat_f[f].sem, xhat_f[f].at(b, 1))
                for c in range(C):
                    turn(tokens, bank[t0 + c], c).then_inc(f_turned[f].sem, 1)
                pe.wait_ge(ft_done[f].sem, ft_done[f].at(b, C))
                for tb in range(TB):
                    for c in range(C):
                        last = mm(bank[low][:, tb * LR:(tb + 1) * LR], xt[:, c, tb * P:(tb + 1) * P], wdown[:, c, :],
                                  start=(c == 0), stop=(c == C - 1))
                last.then_inc(low_ready[f].sem, 1)
                for c in range(C):
                    for tb in range(TB):
                        o = (tb % 2) * D
                        mm(bank[o0 + tb // 2][:, o:o + D], xt[:, c, tb * P:(tb + 1) * P], wbase[:, c, :],
                           start=(c == 0 and tb % 2 == 0), stop=False, skip_group_check=True)

            def ffn_out(b, f):
                o0, turned = FFN[f][4:6]
                pe.wait_ge(hw_done[f].sem, hw_done[f].at(b, 1))
                for tb in range(TB):
                    last = nc.tensor.transpose(bank[turned][0:(E + 1) * R, tb * P:(tb + 1) * P], hw[:, tb, :],
                                               ident[:, :])
                last.then_inc(hw_turned[f].sem, 1)
                pe.wait_ge(hwt_done[f].sem, hwt_done[f].at(b, 1))
                for j in range(2):
                    for tb in (2 * j, 2 * j + 1):
                        o = (tb % 2) * D
                        last = mm(bank[o0 + j][:, o:o + D], hw_t[:, tb * P:(tb + 1) * P], wup[:, :],
                                  start=False, stop=True, skip_group_check=True)
                    last.then_inc(f_ready[f].sem, 1)

            def ssm_gate(b):
                pe.wait_ge(xhat_s.sem, xhat_s.at(b, 1))
                for c in range(C):
                    turn(tok, bank[c], c).then_inc(s_turned.sem, 1)
                pe.wait_ge(xst_done.sem, xst_done.at(b, C))
                for g, dst in enumerate((bank[2], bank[5])):
                    by_columns(dst[:, :], wg, xs_t[:, :, TAPS - 1:], g).then_inc(g_ready.sem, 1)

            def ssm_project(b, beside):
                pe.wait_ge(xc_done.sem, xc_done.at(b, C))
                if beside:
                    pe.wait_ge(ft_done[1].sem, ft_done[1].at(b - 1, C))
                pe.wait_ge(g_done.sem, g_done.at(b, 1))
                for c in range(C):
                    last = mm(bank[6][0:6 * NS, :], wbc[:, c, :, :], xc[:, c, :], start=(c == 0), stop=(c == C - 1))
                last.then_inc(bc_ready.sem, 1)
                for g, dst in enumerate((bank[7], bank[2])):
                    by_columns(dst[:, :], wd, xc, g).then_inc(d_ready.sem, 1)
                pe.wait_ge(bc_done.sem, bc_done.at(b, 1))
                for n in range(B_FIRST):
                    spread_b(b, n)

            def spread_b(b, n):
                pe.wait_ge(b_done.sem, b_done.at(b, n - 1))
                mm(bank[n % 2][:, :], onehot[:, n, :], bcs[:, :], start=True, stop=True).then_inc(b_ready.sem, 1)

            def spread_c(b, n):
                pe.wait_ge(hc_done.sem, hc_done.at(b, n))
                mm(bank[5][:, :], onehot[:, NS + n, :], bcs[:, :], start=True, stop=True).then_inc(c_ready.sem, 1)

            def sum_states(b, n):
                pe.wait_ge(hc_done.sem, hc_done.at(b, n + 1))
                for tb in range(TB):
                    for c in range(C):
                        o = (tb % 2) * D + c * P
                        last = mm(bank[6 + tb // 2][:, o:o + P], hc[:, n % 2, c, tb * P:(tb + 1) * P], ident[:, :],
                                  start=(n == 0 and tb % 2 == 0 and c == 0), stop=(n == NS - 1),
                                  is_transpose=True, skip_group_check=True)
                last.then_inc(y_ready.sem, 1)

            def turn_y(b, beside):
                pe.wait_ge(y_done.sem, y_done.at(b, 2))
                if beside:
                    pe.wait_ge(x1_done.sem, x1_done.at(b + 1, 2))
                for c in range(C):
                    turn(y_tok, bank[4 + c], c).then_inc(y_turned.sem, 1)

            def ssm_out(b, v_of):
                pe.wait_ge(yg_done.sem, yg_done.at(b, C))
                if v_of is not None:
                    pe.wait_ge(v_done.sem, v_done.at(v_of, 2))
                for j in range(2):
                    by_tokens(bank[6 + j], gate, wso, j).then_inc(so_ready.sem, 1)

            def slots(i, attn, ssm):
                if ssm:
                    s = i - 1
                    pe.wait_ge(u_done.sem, u_done.at(s, 1))
                    spread_c(s, 0)
                for k in range(NS):
                    units = range(MU * k, MU * (k + 1)) if attn and k < MSLOTS else ()
                    for g in units[:MU // 2]:
                        max_unit(i, g)
                    if ssm:
                        if k:
                            sum_states(s, k - 1)
                            spread_c(s, k)
                        for n in B_SLOT.get(k, ()):
                            spread_b(s, n)
                    for g in units[MU // 2:]:
                        max_unit(i, g)
                    if attn and k == MSLOTS:
                        max_rows(i)
                    if attn and k == HSLOT - 1:
                        if ssm:
                            pe.wait_ge(b_done.sem, b_done.at(s, NS))
                        for un in range(UN):
                            score_unit(i, un)
                    j = k - HSLOT
                    if attn and 0 <= j < HP:
                        if j + 1 < HP:
                            for un in range(UN):
                                score_unit(i, UN * (j + 1) + un)
                        values(i, j)
                if ssm:
                    sum_states(s, NS - 1)

            def finish(i, attn, ssm, ahead):
                if attn:
                    turn_ao(i)
                if ahead:
                    turn_xn(i + 1, False)
                if attn:
                    attn_out(i)
                if ahead:
                    if ssm:
                        pe.wait_ge(y_done.sem, y_done.at(i - 1, 2))
                    project_qkv(i + 1, False)
                if ssm:
                    turn_y(i - 1, attn)
                if attn:
                    if ahead:
                        pe.wait_ge(qk_biased.sem, qk_biased.at(i + 1, 2 * C))
                    if ssm:
                        pe.wait_ge(yg_done.sem, yg_done.at(i - 1, C))
                    else:
                        pe.wait_ge(x1_done.sem, x1_done.at(i, 2))
                    ffn_in(i, 0)
                if ssm:
                    ssm_out(i - 1, i + 1 if ahead else None)
                if attn:
                    ffn_out(i, 0)
                    ssm_gate(i)
                if ssm:
                    ffn_in(i - 1, 1)
                    ffn_out(i - 1, 1)
                if attn:
                    ssm_project(i, ssm)

            for _n in range(2):
                pe.sem_inc(pv_ready.sem, 1)
                pe.sem_inc(y_ready.sem, 1)
            pe.wait_ge(w_in, 16 * N_LOADS)
            pe.wait_ge(pool_const, 1)
            pe.wait_ge(dve_const, 1)
            turn_xn(0, True)
            project_qkv(0, True)
            slots(0, True, False)
            finish(0, True, False, True)
            with pe.Fori(1, NB - 1) as i:
                slots(i, True, True)
                finish(i, True, True, True)
            slots(NB - 1, True, True)
            finish(NB - 1, True, True, False)
            slots(NB, False, True)
            finish(NB, False, True, False)

        @block.scalar
        def _(act):
            A = nc.scalar.activation

            def copies(b, ready, done, bank0, dst):
                for c in range(C):
                    act.wait_ge(ready.sem, ready.at(b, c + 1))
                    nc.scalar.copy(dst[:, c, :], bank[bank0 + c][:, :]).then_inc(done.sem, 1)

            def split_qk(b):
                for g in range(2 * C):
                    act.wait_ge(qk_ready.sem, qk_ready.at(b, g + 1))
                    scale = HD ** -0.5 if g < C else 1.0
                    A(qkf[:, g, :], bank[g][:, :], ACT.Identity, bias=bqk[:, g:g + 1], scale=scale)
                    A(parts[:, 0, g, :], bank[g][:, :], ACT.Identity, bias=bqk[:, g:g + 1],
                      scale=scale).then_inc(qk_biased.sem, 1)

            def split_mid(b):
                for j in range(2):
                    act.wait_ge(high_off.sem, high_off.at(b, j + 1))
                    nc.scalar.copy(parts[:, 1, C * j:C * j + C, :], qkf[:, C * j:C * j + C, :]).then_inc(mid_done.sem, 1)

            def exp_unit(b, g):
                j, un = divmod(g, UN)
                if un == 0:
                    act.wait_ge(pv_ready.sem, pv_ready.at(b, j - 1))
                act.wait_ge(st_ready.sem, st_ready.at(b, g + 1))
                A(pt_v[:, j % 2, un, :], bank[g % 2][:, :], ACT.Exp).then_inc(exp_done.sem, 1)

            def ffn_exp(b, f):
                act.wait_ge(lg_done[f].sem, lg_done[f].at(b, 1))
                A(ex[:, :, :], lg[:, :, :], ACT.Exp).then_inc(ex_done[f].sem, 1)

            def ffn_turned(b, f):
                act.wait_ge(hw_turned[f].sem, hw_turned[f].at(b, 1))
                nc.scalar.copy(hw_t, bank[FFN[f][5]][0:(E + 1) * R, :]).then_inc(hwt_done[f].sem, 1)

            def ssm_tanh(b):
                for c, src in enumerate((bank[2], bank[5])):
                    act.wait_ge(g_ready.sem, g_ready.at(b, c + 1))
                    A(gate[:, c, :], src[:, :], ACT.Tanh, bias=bg_c[:, c:c + 1], scale=0.5).then_inc(g_done.sem, 1)
                for c in range(C):
                    act.wait_ge(conv_done.sem, conv_done.at(b, c + 1))
                    A(sp_t[:, c, :], xc[:, c, :], ACT.Tanh).then_inc(tanh_done.sem, 1)

            def ssm_softplus(b):
                act.wait_ge(bc_ready.sem, bc_ready.at(b, 1))
                nc.scalar.copy(bcs[:, :], bank[6][0:6 * NS, :]).then_inc(bc_high.sem, 1)
                for c, src in enumerate((bank[7], bank[2])):
                    act.wait_ge(d_ready.sem, d_ready.at(b, c + 1))
                    A(dt[:, c, :], src[:, :], ACT.Relu, bias=bd_c[:, c:c + 1])
                    last = A(sp_t[:, c, :], src[:, :], ACT.Abs, bias=bd_c[:, c:c + 1])
                last.then_inc(act_s.sem, 1)
                act.wait_ge(act_s.sem, act_s.next(b))
                A(sp_t[:, :, :], sp_t[:, :, :], ACT.Exp, scale=-1.0).then_inc(act_s.sem, 1)
                act.wait_ge(act_s.sem, act_s.next(b))
                A(sp_t[:, :, :], sp_t[:, :, :], ACT.Ln, bias=1.0).then_inc(sp_done.sem, 1)
                for n in range(B_FIRST):
                    copy_b(b, n)

            def copy_b(b, n):
                act.wait_ge(b_ready.sem, b_ready.at(b, n + 1))
                if n >= RB:
                    act.wait_ge(inp_ready.sem, inp_ready.at(b, n - RB + 1))
                nc.scalar.copy(b_all[:, n % RB, :], bank[n % 2][:, :]).then_inc(b_done.sem, 1)

            def decays(b, n):
                if n == 0:
                    act.wait_ge(u_done.sem, u_done.at(b, 1))
                act.wait_ge(scan_done.sem, scan_done.at(b, n - 1))
                for c in range(C):
                    last = A(dec[:, n % 2, c, 1:T], dt[:, c, 1:T], ACT.Exp, scale=a_neg[:, c, n:n + 1])
                last.then_inc(dec_ready.sem, 1)

            def slots(i, attn, ssm):
                if ssm:
                    s = i - 1
                    decays(s, 0)
                for k in range(NS):
                    if ssm:
                        if k + 1 < NS:
                            decays(s, k + 1)
                        for n in B_SLOT.get(k, ()):
                            copy_b(s, n)
                    j = k - HSLOT
                    if attn and 0 <= j < HP:
                        for un in range(UN):
                            exp_unit(i, UN * j + un)

            def finish(i, attn, ssm, ahead):
                if ssm:
                    act.wait_ge(y_ready.sem, y_ready.at(i - 1, NS))
                    for j in range(2):
                        nc.scalar.copy(y_tok[:, 2 * j:2 * j + 2, :].rearrange("p t d -> p (t d)"),
                                       bank[6 + j][:, :]).then_inc(y_done.sem, 1)
                if attn:
                    copies(i, ao_turned, aot_done, 0, xt_a)
                if ahead:
                    copies(i + 1, xn_turned, xnt_done, 2, xt_b)
                    split_qk(i + 1)
                if attn:
                    copies(i, f_turned[0], ft_done[0], 0, xt_a)
                    ffn_exp(i, 0)
                if ahead:
                    split_mid(i + 1)
                if attn:
                    ffn_turned(i, 0)
                    copies(i, s_turned, xst_done, 0, xs_t[:, :, TAPS - 1:])
                if ssm:
                    copies(i - 1, f_turned[1], ft_done[1], 6, xt_b)
                if attn:
                    ssm_tanh(i)
                if ssm:
                    ffn_exp(i - 1, 1)
                    ffn_turned(i - 1, 1)
                if attn:
                    ssm_softplus(i)

            for _n in range(2):
                act.sem_inc(exp_done.sem, 1)
                act.sem_inc(b_done.sem, 1)
            act.wait_ge(w_in, 16 * N_LOADS)
            A(a_neg[:, :, :], a_neg[:, :, :], ACT.Exp).then_inc(act_const, 1)
            act.wait_ge(dve_const, 1)
            copies(0, xn_turned, xnt_done, 2, xt_b)
            split_qk(0)
            split_mid(0)
            slots(0, True, False)
            finish(0, True, False, True)
            with act.Fori(1, NB - 1) as i:
                slots(i, True, True)
                finish(i, True, True, True)
            slots(NB - 1, True, True)
            finish(NB - 1, True, True, False)
            slots(NB, False, True)
            finish(NB, False, True, False)

        @block.vector
        def _(dve):
            V = nc.vector

            def normalise(b, src, steps, var, rsq, done, dst, mul, add):
                for tb in range(TB):
                    last = V.bn_stats(st[:, tb, :], src[:, tb, :])
                last.then_inc(steps.sem, 1)
                dve.wait_ge(steps.sem, steps.next(b))
                dve.sem_inc(waited, 1)
                for tb in range(TB):
                    last = V.bn_aggr(mv[:, tb, :], st[:, tb, :])
                last.then_inc(steps.sem, 1)
                dve.wait_ge(steps.sem, steps.next(b))
                V.tensor_scalar(va[:, :], mv[:, :, 1], mul, add, ALU.mult, ALU.add).then_inc(var.sem, 1)
                dve.wait_ge(rsq.sem, rsq.at(b, 1))
                V.scalar_tensor_tensor(nm[:, :], mv[:, :, 0], -1.0, rs[:, :], ALU.mult, ALU.mult).then_inc(steps.sem, 1)
                dve.wait_ge(steps.sem, steps.next(b))
                for tb in range(TB):
                    last = V.tensor_scalar(dst[:, tb, :], src[:, tb, :], rs[:, tb:tb + 1], nm[:, tb:tb + 1],
                                           ALU.mult, ALU.add)
                last.then_inc(done.sem, 1)

            def attn_normalise(b):
                dve.wait_ge(x_loaded.sem, x_loaded.at(b, 1))
                e1, e2 = 1e-5, 1e-6
                normalise(b, x_in, dve_a, var_a, rs_a, xhat_a, tok, 1.0 + e2, e1 * e2)

            def attn_v(b):
                for j in range(2):
                    dve.wait_ge(v_ready.sem, v_ready.at(b, j + 1))
                    V.tensor_tensor(v_sb[:, 2 * j:2 * j + 2, :, 0:HD],
                                    bank[6 + j][:, :].rearrange("p (t h i) -> p t h i", t=2, h=H),
                                    rows(bv_row, 2).rearrange("p t (h i) -> p t h i", h=H),
                                    ALU.add).then_inc(v_done.sem, 1)

            def maximum(b, g):
                dve.wait_ge(mx_ready.sem, mx_ready.at(b, g + 1))
                src = bank[2 + g % 2][:, :].rearrange("p (k n) -> p k n", k=TB)
                V.tensor_reduce(mxp[:, g // UN, g % UN, :], src, AXX, ALU.max).then_inc(mx_used.sem, 1)

            def max_columns(b):
                dve.wait_ge(mx_used.sem, mx_used.at(b, HP * UN))

                def neg(qb, src):
                    dst = negm[:, qb, :].rearrange("p (j h) -> p j h", h=2)
                    return V.tensor_reduce(dst, src, AXX, ALU.max, negate=True)

                neg(3, mxp[:, :, 0:3:2, :])
                neg(2, mxp[:, :, 1:4:2, 0:3])
                neg(0, mxp[:, :, 1:4:2, 3:4])
                neg(1, mxp[:, :, 4, :].rearrange("p j (h k) -> p j h k", h=2)).then_inc(negm_done.sem, 1)

            def max_rows(b):
                dve.wait_ge(mx_ready.sem, mx_ready.at(b, HP * UN + 1))
                V.tensor_copy(mrow[:, 0, :], bank[2][0:H, :]).then_inc(dve_m.sem, 1)
                dve.wait_ge(dve_m.sem, dve_m.next(b))
                V.tensor_tensor(mrow[:, 1, :], bank[2][0:H, :], mrow[:, 0, :], ALU.subtract).then_inc(mrow_done.sem, 1)
                dve.wait_ge(mrow_done.sem, mrow_done.at(b, 1))
                dve.sem_inc(mx_used.sem, 2)

            def head_norm(b, j):
                dve.wait_ge(pv_ready.sem, pv_ready.at(b, j + 1))
                pv = bank[4][:, 0:2 * TB * (HD + 1)].rearrange("p (g i) -> p g i", i=HD + 1)
                V.reciprocal(rc[:, :], pv[:, :, HD]).then_inc(dve_h.sem, 1)
                dve.wait_ge(dve_h.sem, dve_h.next(b))
                for hh in range(2):
                    h = 2 * j + hh
                    last = V.tensor_tensor(ao[:, :, h * HD:(h + 1) * HD], pv[:, hh * TB:(hh + 1) * TB, 0:HD],
                                           rc[:, hh * TB:(hh + 1) * TB, None].to_broadcast([P, TB, HD]), ALU.mult)
                last.then_inc(pv_used.sem, 1)

            def add_out(b, ready, done, bank0, src, dst):
                for j in range(2):
                    dve.wait_ge(ready.sem, ready.at(b, j + 1))
                    V.tensor_tensor(dst[:, 2 * j:2 * j + 2, :],
                                    bank[bank0 + j][:, :].rearrange("p (t d) -> p t d", t=2),
                                    src[:, 2 * j:2 * j + 2, :], ALU.add).then_inc(done.sem, 1)

            def ffn_normalise(b, f):
                if f == 0:
                    dve.wait_ge(x1_done.sem, x1_done.at(b, 2))
                else:
                    dve.wait_ge(x3_done.sem, x3_done.at(b, 2))
                normalise(b, (res_a, res_s)[f], dve_n[f], var_f[f], rs_f[f], xhat_f[f], FFN[f][0], 1.0, 1e-5)

            def router_in(b, f):
                low = bank[FFN[f][3]][:, 0:TB * LR].rearrange("p (t l) -> p t l", t=TB)
                steps = dve_r[f]
                dve.wait_ge(low_ready[f].sem, low_ready[f].at(b, 1))
                V.tensor_tensor(lg[:, :, :], low[:, :, LR - E:LR], rb_row[:, None, :].to_broadcast([P, TB, E]),
                                ALU.add).then_inc(steps.sem, 1)
                dve.wait_ge(steps.sem, steps.next(b))
                V.tensor_reduce(red[:, 0, :], lg[:, :, :], AXX, ALU.max).then_inc(steps.sem, 1)
                dve.wait_ge(steps.sem, steps.next(b))
                V.tensor_tensor(lg[:, :, :], lg[:, :, :], red[:, 0, :, None].to_broadcast([P, TB, E]),
                                ALU.subtract).then_inc(lg_done[f].sem, 1)

            def router_out(b, f):
                low = bank[FFN[f][3]][:, 0:TB * LR].rearrange("p (t l) -> p t l", t=TB)
                steps = dve_r[f]
                dve.wait_ge(ex_done[f].sem, ex_done[f].at(b, 1))
                mine = ex[:, :, :, None].to_broadcast([P, TB, E, E])
                other = ex[:, :, None, :].to_broadcast([P, TB, E, E])
                V.tensor_tensor(cmp_b[:, :, :, :], other, mine, ALU.is_equal).then_inc(steps.sem, 1)
                V.tensor_tensor(cmp_a[:, :, :, :], other, mine, ALU.is_gt)
                dve.wait_ge(steps.sem, steps.next(b))
                V.tensor_tensor(cmp_b[:, :, :, :], cmp_b[:, :, :, :],
                                below[:, None, :, :].to_broadcast([P, TB, E, E]), ALU.mult).then_inc(steps.sem, 1)
                V.tensor_reduce(red[:, 1, :], ex[:, :, :], AXX, ALU.add)
                dve.wait_ge(steps.sem, steps.next(b))
                V.tensor_tensor(cmp_a[:, :, :, :], cmp_a[:, :, :, :], cmp_b[:, :, :, :],
                                ALU.add).then_inc(steps.sem, 1)
                dve.wait_ge(steps.sem, steps.next(b))
                V.tensor_reduce(rank[:, :, :], cmp_a[:, :, :, :], AXX, ALU.add).then_inc(steps.sem, 1)
                dve.wait_ge(steps.sem, steps.next(b))
                V.scalar_tensor_tensor(rank[:, :, :], rank[:, :, :], 1.5, ex[:, :, :], ALU.is_lt,
                                       ALU.mult).then_inc(steps.sem, 1)
                dve.wait_ge(steps.sem, steps.next(b))
                V.tensor_reduce(red[:, 2, :], rank[:, :, :], AXX, ALU.add).then_inc(steps.sem, 1)
                dve.wait_ge(steps.sem, steps.next(b))
                V.scalar_tensor_tensor(red[:, 3, :], red[:, 1, :], 1e-6, red[:, 2, :], ALU.mult,
                                       ALU.add).then_inc(steps.sem, 1)
                dve.wait_ge(steps.sem, steps.next(b))
                V.reciprocal(red[:, 3, :], red[:, 3, :]).then_inc(steps.sem, 1)
                dve.wait_ge(steps.sem, steps.next(b))
                V.tensor_tensor(wts[:, :, 1:], rank[:, :, :], red[:, 3, :, None].to_broadcast([P, TB, E]),
                                ALU.mult).then_inc(steps.sem, 1)
                dve.wait_ge(steps.sem, steps.next(b))
                V.tensor_tensor(hw.rearrange("p t (e r) -> p t e r", r=R),
                                low[:, :, 0:(E + 1) * R].rearrange("p t (e r) -> p t e r", r=R),
                                wts[:, :, :, None].to_broadcast([P, TB, E + 1, R]),
                                ALU.mult).then_inc(hw_done[f].sem, 1)

            def ffn_add(b, f):
                dve.wait_ge(bias_f[f].sem, bias_f[f].at(b, 1))
                if f == 0:
                    add_out(b, f_ready[0], f_done[0], FFN[0][4], res_a, res_a)
                else:
                    dve.wait_ge(x_stored.sem, x_stored.at(b, 0))
                    add_out(b, f_ready[1], f_done[1], FFN[1][4], res_s, x_out)

            def ssm_normalise(b):
                dve.wait_ge(f_done[0].sem, f_done[0].at(b, 2))
                normalise(b, res_a, dve_n[2], var_s, rs_s, xhat_s, tok, 1.0, 1e-5)

            def ssm_conv(b):
                dve.wait_ge(xst_done.sem, xst_done.at(b, C))
                for k in range(TAPS):
                    for c in range(C):
                        if k == 0:
                            last = V.tensor_scalar(xc[:, c, :], xs_t[:, c, 0:T], cw[:, c, 0:1], cb[:, c:c + 1],
                                                   ALU.mult, ALU.add)
                        else:
                            last = V.scalar_tensor_tensor(xc[:, c, :], xs_t[:, c, k:k + T], cw[:, c, k:k + 1],
                                                          xc[:, c, :], ALU.mult, ALU.add)
                        if k == TAPS - 1:
                            last.then_inc(conv_done.sem, 1)
                    if k < TAPS - 1:
                        last.then_inc(dve_s.sem, 1)
                        dve.wait_ge(dve_s.sem, dve_s.next(b))

            def ssm_silu(b):
                for c in range(C):
                    dve.wait_ge(tanh_done.sem, tanh_done.at(b, c + 1))
                    V.scalar_tensor_tensor(xc[:, c, :], sp_t[:, c, :], 1.0, xc[:, c, :], ALU.add,
                                           ALU.mult).then_inc(xc_done.sem, 1)

            def ssm_bc(b):
                dve.wait_ge(bc_high.sem, bc_high.at(b, 1))
                V.tensor_tensor(bcr[:, :], bank[6][0:6 * NS, :], bcs[:, :], ALU.subtract).then_inc(dve_s.sem, 1)
                dve.wait_ge(dve_s.sem, dve_s.next(b))
                V.tensor_copy(bcs[2 * NS:4 * NS, :], bcr[2 * NS:4 * NS, :])
                V.tensor_copy(bcs[4 * NS:6 * NS, :], bcr[4 * NS:6 * NS, :]).then_inc(dve_s.sem, 1)
                dve.wait_ge(dve_s.sem, dve_s.next(b))
                V.tensor_tensor(bcs[4 * NS:6 * NS, :], bcr[4 * NS:6 * NS, :], bcs[4 * NS:6 * NS, :],
                                ALU.subtract).then_inc(bc_done.sem, 1)

            def scan(b, n):
                dve.wait_ge(dec_ready.sem, dec_ready.at(b, n + 1))
                dve.wait_ge(inp_ready.sem, inp_ready.at(b, n + 1))
                dve.wait_ge(y_ready.sem, y_ready.at(b, n - 1))
                h, d, u_b = (t[:, n % 2, :, :].rearrange("p c t -> p (c t)") for t in (hc, dec, inp))
                V.tensor_tensor_scan(h, d, u_b, 0.0, ALU.mult, ALU.add).then_inc(scan_done.sem, 1)

            def times_c(b, n):
                dve.wait_ge(scan_done.sem, scan_done.at(b, n + 1))
                dve.wait_ge(c_ready.sem, c_ready.at(b, n + 1))
                V.tensor_tensor(hc[:, n % 2, :, :], hc[:, n % 2, :, :],
                                bank[5][:, None, :].to_broadcast([P, C, T]), ALU.mult).then_inc(hc_done.sem, 1)

            def gate_y(b):
                for c in range(C):
                    dve.wait_ge(y_turned.sem, y_turned.at(b, c + 1))
                    V.scalar_tensor_tensor(gate[:, c, :], gate[:, c, :], 1.0, bank[4 + c][:, :],
                                           ALU.add, ALU.mult).then_inc(yg_done.sem, 1)

            def slots(i, attn, ssm, ahead):
                s = i - 1
                for k in range(NS):
                    units = range(MU * k, MU * (k + 1)) if attn and k < MSLOTS else ()
                    if ssm:
                        scan(s, k)
                    for g in units[:MU // 2]:
                        maximum(i, g)
                    if ssm:
                        times_c(s, k)
                    for g in units[MU // 2:]:
                        maximum(i, g)
                    if attn and k == MSLOTS - 1:
                        max_columns(i)
                    if attn and k == MSLOTS:
                        max_rows(i)
                    j = k - HSLOT - 1
                    if attn and 0 <= j < HP:
                        head_norm(i, j)
                    if ahead and k == LN_SLOT:
                        attn_normalise(i + 1)

            def finish(i, attn, ssm, ahead):
                s = i - 1
                if attn:
                    dve.wait_ge(res_done.sem, res_done.at(i, 1))
                    add_out(i, wo_ready, x1_done, 4, res_a, res_a)
                    ffn_normalise(i, 0)
                if ahead:
                    attn_v(i + 1)
                if ssm:
                    gate_y(s)
                if attn:
                    router_in(i, 0)
                if ssm:
                    dve.wait_ge(bias_s.sem, bias_s.at(s, 1))
                    add_out(s, so_ready, x3_done, 6, res_s, res_s)
                if attn:
                    router_out(i, 0)
                    ffn_add(i, 0)
                    ssm_normalise(i)
                if ssm:
                    ffn_normalise(s, 1)
                if attn:
                    ssm_conv(i)
                if ssm:
                    router_in(s, 1)
                if attn:
                    ssm_silu(i)
                if ssm:
                    router_out(s, 1)
                    ffn_add(s, 1)
                if attn:
                    ssm_bc(i)

            V.memset(dec[:, :, :, :], 0.0)
            V.memset(xs_t[:, :, 0:TAPS - 1], 0.0)
            V.memset(v_sb[:, :, :, HD:HD + 1], 1.0)
            V.memset(sk[KS:KS + 2, :, :], 1.0)
            V.memset(wts[:, :, :], 1.0)
            V.memset(half[:, :], -0.5)
            for t in (mx_used, scan_done):
                dve.sem_inc(t.sem, 1)
                dve.sem_inc(t.sem, 1)
            dve.sem_inc(pv_used.sem, 1)
            dve.sem_inc(hc_done.sem, 1)
            dve.wait_ge(w_in, 16 * N_LOADS)
            dve.wait_ge(act_const, 1)
            dve.wait_ge(pool_const, 1)
            V.tensor_scalar(a_neg[:, :, :], a_neg[:, :, :], -1.0, None, ALU.mult)
            V.tensor_scalar(bqk[:, 0:C], bqk[:, 0:C], HD ** -0.5, None, ALU.mult)
            V.tensor_scalar(bg_c[:, :], bg_c[:, :], 0.5, None, ALU.mult)
            V.tensor_scalar(cb[:, :], cb[:, :], 0.5, None, ALU.mult)
            V.tensor_scalar(cw[:, :, :], cw[:, :, :], 0.5, None, ALU.mult)
            V.tensor_copy(ident_bf[:, :], ident[:, :])
            V.tensor_scalar(wso[:, :, :], wso[:, :, :], 0.5, None, ALU.mult).then_inc(dve_const_step, 1)
            dve.wait_ge(dve_const_step, 1)
            dve.sem_inc(dve_const, 1)
            attn_normalise(0)
            attn_v(0)
            slots(0, True, False, True)
            finish(0, True, False, True)
            with dve.Fori(1, NB - 1) as i:
                slots(i, True, True, True)
                finish(i, True, True, True)
            slots(NB - 1, True, True, False)
            finish(NB - 1, True, True, False)
            slots(NB, False, True, False)
            finish(NB, False, True, False)

        @block.gpsimd
        def _(pool):
            G = nc.gpsimd

            def rsqrt(b, var, rsq):
                pool.wait_ge(var.sem, var.at(b, 1))
                G.tensor_tensor(rs[:, :], va[:, :], half[:, :], ALU.pow).then_inc(rsq.sem, 1)

            def weigh(b):
                rsqrt(b, var_a, rs_a)
                pool.wait_ge(xhat_a.sem, xhat_a.at(b, 1))
                G.tensor_tensor(xn[:, :, :], tok[:, :, :], rows(w_row), ALU.mult).then_inc(xn_done.sem, 1)

            def residual(b):
                pool.wait_ge(xn_done.sem, xn_done.at(b, 1))
                G.tensor_tensor(res_a[:, :, :], x_in[:, :, :], xn[:, :, :], ALU.add).then_inc(x_used.sem, 1)
                pool.wait_ge(x_used.sem, x_used.at(b, 1))
                G.tensor_tensor(res_a[:, :, :], res_a[:, :, :], rows(bo_row), ALU.add).then_inc(res_done.sem, 1)

            def split_high(b):
                for j in range(2):
                    pool.wait_ge(qk_biased.sem, qk_biased.at(b, C * (j + 1)))
                    half_qk = qkf[:, C * j:C * j + C, :]
                    G.tensor_tensor(half_qk, half_qk, parts[:, 0, C * j:C * j + C, :],
                                    ALU.subtract).then_inc(high_off.sem, 1)

            def split_low(b):
                for j in range(2):
                    pool.wait_ge(mid_done.sem, mid_done.at(b, j + 1))
                    G.tensor_tensor(parts[:, 2, C * j:C * j + C, :], qkf[:, C * j:C * j + C, :],
                                    parts[:, 1, C * j:C * j + C, :], ALU.subtract).then_inc(low_done.sem, 1)

            def ffn_bias(b, f):
                res = (res_a, res_s)[f]
                pool.wait_ge(xhat_f[f].sem, xhat_f[f].at(b, 1))
                G.tensor_tensor(res[:, :, :], res[:, :, :], rows(bb_row), ALU.add).then_inc(bias_f[f].sem, 1)

            def ssm_step(b):
                pool.wait_ge(sp_done.sem, sp_done.at(b, 1))
                G.tensor_tensor(dt[:, :, :], dt[:, :, :], sp_t[:, :, :], ALU.add).then_inc(u_done.sem, 1)
                pool.wait_ge(u_done.sem, u_done.at(b, 1))
                G.tensor_tensor(u[:, :, :], dt[:, :, :], xc[:, :, :], ALU.mult).then_inc(u_done.sem, 1)
                pool.wait_ge(u_done.sem, u_done.at(b, 2))

            def ssm_residual(b, beside):
                pool.wait_ge(xhat_s.sem, xhat_s.at(b, 1))
                if beside:
                    pool.wait_ge(f_done[1].sem, f_done[1].at(b - 1, 2))
                G.tensor_tensor(res_s[:, :, :], res_a[:, :, :], rows(bso_row), ALU.add).then_inc(bias_s.sem, 1)
                pool.wait_ge(bias_s.sem, bias_s.at(b, 1))

            def inputs(b, n):
                pool.wait_ge(b_done.sem, b_done.at(b, n + 1))
                pool.wait_ge(scan_done.sem, scan_done.at(b, n - 1))
                G.tensor_tensor(inp[:, n % 2, :, :], u[:, :, :],
                                b_all[:, n % RB:n % RB + 1, :].to_broadcast([P, C, T]),
                                ALU.mult).then_inc(inp_ready.sem, 1)

            def slots(i, ssm, ahead):
                for k in range(NS):
                    if ssm:
                        inputs(i - 1, k)
                    if ahead and k == LN_SLOT + 1:
                        weigh(i + 1)

            def finish(i, attn, ssm, ahead):
                if attn:
                    rsqrt(i, var_f[0], rs_f[0])
                    ffn_bias(i, 0)
                if ahead:
                    split_high(i + 1)
                    split_low(i + 1)
                if attn:
                    rsqrt(i, var_s, rs_s)
                if ssm:
                    rsqrt(i - 1, var_f[1], rs_f[1])
                    ffn_bias(i - 1, 1)
                if attn:
                    ssm_step(i)
                    ssm_residual(i, ssm)
                if ahead:
                    residual(i + 1)

            G.memset(ident[:, :], 0.0)
            G.memset(mask_qk[:, :], 0.0)
            G.memset(mask_kq[:, :], 0.0)
            G.memset(below[:, :, :], 1.0)
            G.memset(onehot[:, :, :], 0.0).then_inc(pool_const_step, 1)
            pool.wait_ge(pool_const_step, 1)
            G.affine_select(out=ident[:, :], in_=ident[:, :], compare_op=ALU.not_equal, fill=1.0, base=0,
                            pattern=[[-1, P]], channel_multiplier=1)
            G.affine_select(out=mask_qk[:, :], in_=mask_qk[:, :], compare_op=ALU.is_ge, fill=BIG, base=0,
                            pattern=[[-1, P]], channel_multiplier=1)
            G.affine_select(out=mask_kq[:, :], in_=mask_kq[:, :], compare_op=ALU.is_ge, fill=BIG, base=0,
                            pattern=[[1, P]], channel_multiplier=-1)
            G.affine_select(out=below[:, :, :], in_=below[:, :, :], compare_op=ALU.is_gt, fill=0.0, base=0,
                            pattern=[[1, E], [-1, E]], channel_multiplier=0)
            for j in range(3):
                G.affine_select(out=onehot[:, :, :], in_=onehot[:, :, :], compare_op=ALU.not_equal, fill=1.0,
                                base=-2 * NS * j, pattern=[[-1, 2 * NS], [0, P]],
                                channel_multiplier=1).then_inc(pool_const_step, 1)
                pool.wait_ge(pool_const_step, 2 + j)
            pool.sem_inc(pool_const, 1)
            pool.sem_inc(x_used.sem, 1)
            pool.wait_ge(w_in, 16 * N_LOADS)
            pool.wait_ge(dve_const, 1)
            weigh(0)
            split_high(0)
            split_low(0)
            residual(0)
            slots(0, False, True)
            finish(0, True, False, True)
            with pool.Fori(1, NB - 1) as i:
                slots(i, True, True)
                finish(i, True, True, True)
            slots(NB - 1, True, False)
            finish(NB - 1, True, True, False)
            slots(NB, True, False)
            finish(NB, False, True, False)

        assert all(t.n % t.per == 0 for t in tallies)


def kernel(**inputs):
    import numpy as np
    import concourse.bacc as bacc
    from concourse.bass_utils import run_bass_kernel_spmd

    g = {k: np.asarray(v) for k, v in inputs.items()}
    a, s, f = "L0_attn_a_", "L0_attn_b_", "L0_ffn_"
    E, R, D = g[f + "routed_A"].shape
    t = np.transpose

    def by_partition(*vectors):
        return t(np.concatenate(vectors).reshape(-1, P))

    arrays = {
        "x": g[a + "x"], "norm_w": g[a + "norm_w"],
        "wqk_t": np.concatenate([t(g[a + "Wq"]), t(g[a + "Wk"])], 1), "bqk": by_partition(g[a + "bq"], g[a + "bk"]),
        "wv_t": t(g[a + "Wv"]), "bv": g[a + "bv"], "wo_t": t(g[a + "Wo"]), "bo": g[a + "bo"],
        "conv_w": g[s + "conv_w"][:, 0, :], "conv_b": by_partition(g[s + "conv_b"]), "wd_t": t(g[s + "Wd"]), "bd": by_partition(g[s + "bd"]),
        "wbc_t": np.concatenate([t(g[s + "Wb"]), t(g[s + "Wc"])], 1), "log_a": g[s + "log_a"],
        "wg_t": t(g[s + "Wg"]), "bg": by_partition(g[s + "bg"]), "wso_t": t(g[s + "Wo"]), "bso": g[s + "bo"],
        "base_t": t(g[f + "base_W"]), "base_b": g[f + "base_b"],
        "down_t": np.concatenate([t(g[f + "shared_A"]), t(g[f + "routed_A"].reshape(E * R, D)), t(g[f + "router_W"])], 1),
        "up_s": np.concatenate([t(g[f + "shared_B"]), t(g[f + "routed_B"], (0, 2, 1)).reshape(E * R, D)], 0),
        "router_b": g[f + "router_b"],
    }
    arrays = {f"in_{k}": np.ascontiguousarray(v) for k, v in arrays.items()}
    nc = bacc.Bacc("TRN2", target_bir_lowering=False, num_devices=1)
    args = [nc.dram_tensor(k, v.shape, mybir.dt.from_np(v.dtype), kind="ExternalInput").ap() for k, v in arrays.items()]
    out = nc.dram_tensor("out", g[a + "x"].shape, F32, kind="ExternalOutput").ap()
    hybrid_block(nc, *args, out)
    r = run_bass_kernel_spmd(nc, [arrays], core_ids=[0])
    return r.results[0]["out"]
```

```python
from contextlib import ExitStack

import concourse.bass as bass
from concourse import mybir

F32 = mybir.dt.float32
BF16 = mybir.dt.bfloat16
ALU = mybir.AluOpType
ACT = mybir.ActivationFunctionType
AXX = mybir.AxisListType.X

P = 128
BIG = -1.0e30


class Tally:

    def __init__(self, sem, per, credit=0, step=1):
        self.sem, self.per, self.credit, self.step = sem, per, credit, step
        self.n = 0

    def at(self, b, n):
        return b * (self.per * self.step) + (n * self.step + self.credit)

    def next(self, b):
        self.n += 1
        return self.at(b, (self.n - 1) % self.per + 1)


def hybrid_block(nc, x, norm_w, wqk_t, bqk_c, wv_t, bv, wo_t, bo, conv_w, conv_b, wd_t, bd, wbc_t,
                 log_a, wg_t, bg, wso_t, bso, base_t, base_b, down_t, up_s, router_b, out):
    NB, T, D = x.shape
    C = D // P
    TB = T // P
    H = 16
    HD = D // H
    NS = log_a.shape[1]
    E = router_b.shape[0]
    R = up_s.shape[0] // (E + 1)
    LR = down_t.shape[1]
    HP = H // 2
    UN = 5
    TAPS = conv_w.shape[1]
    RB = 4
    LEAD = 2
    VW = 32
    HG = 4
    TERMS = [(0, 0), (0, 1), (1, 0), (0, 2), (2, 0), (1, 1)]
    KS = len(TERMS) * HD

    ctx = ExitStack()
    with ctx:
        def sb(name, shape, dt=F32):
            return ctx.enter_context(nc.sbuf_tensor(name, shape, dt))

        def sem(name):
            return ctx.enter_context(nc.semaphore(name))

        def tally(name, per, credit=0, step=1):
            t = Tally(sem(name), per, credit, step)
            tallies.append(t)
            return t

        tallies = []
        bank = [ctx.enter_context(nc.psum_tensor(f"bank{i}", [P, 512], F32)) for i in range(8)]

        ident = sb("ident", [P, P])
        ident_bf = sb("ident_bf", [P, P], BF16)
        mask_qk = sb("mask_qk", [P, P], BF16)
        mask_kq = sb("mask_kq", [P, P], BF16)
        onehot = sb("onehot", [3 * 2 * NS, 2 * NS, P], BF16)
        wqk = sb("wqk", [P, C, 2 * D])
        wv = sb("wv", [P, C, D])
        wo = sb("wo", [P, C, D])
        wd = sb("wd", [P, C, D])
        wg = sb("wg", [P, C, D])
        wso = sb("wso", [P, C, D])
        wbase = sb("wbase", [P, C, D])
        wdown = sb("wdown", [P, C, LR])
        wup = sb("wup", [(E + 1) * R + 1, D])
        wbc = sb("wbc", [P, C, 3, 2 * NS])
        bqk = sb("bqk", [P, 2 * C])
        bd_c = sb("bd_c", [P, C])
        bg_c = sb("bg_c", [P, C])
        cw = sb("cw", [P, C, TAPS])
        cb = sb("cb", [P, C])
        a_neg = sb("a_neg", [P, C, NS])
        w_row = sb("w_row", [P, D])
        bv_row = sb("bv_row", [P, D])
        bo_row = sb("bo_row", [P, D])
        bso_row = sb("bso_row", [P, D])
        rb_row = sb("rb_row", [P, E])
        below = sb("below", [P, E, E])
        half = sb("half", [P, TB])

        x_in = sb("x_in", [P, TB, D])
        res_a = sb("res_a", [P, TB, D])
        res_s = sb("res_s", [P, TB, D])
        tok = sb("tok", [P, TB, D])
        xn = sb("xn", [P, TB, D])
        ao = sb("ao", [P, TB, D])
        y_tok = sb("y_tok", [P, TB, D])
        x_out = sb("x_out", [P, TB, D])
        xt_a = sb("xt_a", [P, C, T])
        xt_b = sb("xt_b", [P, C, T])
        pt = sb("pt", [P, 2 * UN * 512])
        pt_v = pt[:, :].rearrange("p (r u n) -> p r u n", r=2, u=UN)
        qkf = pt[:, 0:2 * C * T].rearrange("p (g t) -> p g t", g=2 * C)
        parts = pt[:, 2 * C * T:5 * C * T].bitcast(BF16).rearrange("p (j g t) -> p j g t", j=3, g=2 * C)
        sq = sb("sq", [KS + 2, H, T], BF16)
        sk = sb("sk", [KS + 2, H, T], BF16)
        v_sb = sb("v_sb", [P, TB, H, VW])
        mxp = sb("mxp", [P, HP, UN, TB])
        negm = sb("negm", [P, TB, H])
        mrow = sb("mrow", [H, 2, T], BF16)
        ot_sb = sb("ot_sb", [P, T])
        rc = sb("rc", [P, TB, HG])
        st = sb("st", [P, TB, 6])
        mv = sb("mv", [P, TB, 2])
        va = sb("va", [P, TB])
        rs = sb("rs", [P, TB])
        nm = sb("nm", [P, TB])
        lg = sb("lg", [P, TB, E])
        ex = sb("ex", [P, TB, E])
        cmp_a = sb("cmp_a", [P, TB, E, E])
        cmp_b = sb("cmp_b", [P, TB, E, E])
        rank = sb("rank", [P, TB, E])
        red = sb("red", [P, 4, TB])
        wts = sb("wts", [P, TB, E + 1])
        xs_t = sb("xs_t", [P, C, TAPS - 1 + T])
        xc = sb("xc", [P, C, T])
        sp_t = sb("sp_t", [P, C, T])
        hw = sb("hw", [P, TB, (E + 1) * R + 1])
        hw_t = sp_t[0:(E + 1) * R + 1, 1, :]
        dt = sb("dt", [P, C, T])
        u = sb("u", [P, C, T])
        gate = sb("gate", [P, C, T])
        y_sum = sb("y_sum", [P, C, T])
        gate_y = sb("gate_y", [P, C, T])
        bcs = sb("bcs", [3 * 2 * NS, T], BF16)
        bcr = ot_sb[0:3 * 2 * NS, :]
        b_all = sb("b_all", [P, RB, T])
        dec = sb("dec", [P, 2, C, T])
        inp = sb("inp", [P, 2, C, T])
        hc = sb("hc", [P, 2, C, T])

        scratch = nc.dram_tensor("qk_parts", [NB, 3, 2 * C, P, T], BF16, kind="Internal").ap()

        FFN = ((tok, xt_a, (1, 7)), (y_tok, xt_b, (1, 4)))

        w_in = sem("weights_loaded")
        pool_const = sem("pool_constants")
        dve_const = sem("dve_constants")
        act_const = sem("act_constants")
        dve_const_step = sem("dve_constant_step")
        pool_const_step = sem("pool_constant_steps")
        waited = sem("waited")

        x_loaded = tally("x_loaded", 1, step=16)
        x_used = tally("x_used", 1, credit=1)
        var_a, rs_a = tally("attn_variance", 1), tally("attn_rsqrt", 1)
        xhat_a = tally("attn_normalised", 1)
        xn_done = tally("xn_done", 1)
        res_done = tally("res_done", 1)
        xn_turned = tally("xn_turned", C)
        xnt_done = tally("xnt_done", C)
        qk_ready = tally("qk_ready", 2 * C)
        qk_biased = tally("qk_biased", 2 * C)
        v_ready = tally("v_ready", 2)
        v_done = tally("v_done", 2)
        high_off = tally("high_parts_off", 2)
        mid_done = tally("middle_parts", 2)
        low_done = tally("low_parts", 2)
        part_stored = tally("part_stored", 3, step=16)
        stacked = tally("stacked", 2 * len(TERMS), step=16)
        mx_ready = tally("scores_for_max", HP * UN + 1)
        mx_used = tally("scores_for_max_used", HP * UN, credit=4)
        negm_done = tally("negm_done", 1)
        mrow_done = tally("mrow_done", 1)
        m_stacked = tally("max_stacked", 2, step=16)
        st_ready = tally("scores_ready", HP * UN)
        exp_done = tally("exp_done", HP * UN, credit=4)
        pt_read = tally("pair_of_exps_read", HP, credit=2)
        ot_done = tally("outputs_by_columns_copied", H // HG)
        pv_ready = tally("pv_ready", H // HG)
        pv_used = tally("pv_used", H // HG)
        ao_turned = tally("ao_turned", C)
        aot_done = tally("aot_done", C)
        wo_ready = tally("wo_ready", 2)
        x1_done = tally("x1_done", 2)
        var_f, rs_f, xhat_f, f_turned, ft_done, low_ready, lg_done, ex_done, hw_done, hw_turned, hwt_done, f_ready, f_done = (
            [tally(f"ffn{f}_{name}", per) for f in range(2)] for name, per in
            (("variance", 1), ("rsqrt", 1), ("normalised", 1), ("turned", C), ("turned_copied", C),
             ("low_rank", 1), ("logits", 1), ("exp", 1), ("weighted", 1), ("weighted_turned", 1), ("weighted_copied", 1),
             ("ready", 2), ("done", 2)))
        x_stored = tally("x_stored", 1, credit=16, step=16)
        var_s, rs_s = tally("ssm_variance", 1), tally("ssm_rsqrt", 1)
        xhat_s = tally("ssm_normalised", 1)
        bias_s = tally("ssm_bias_added", 1)
        s_turned = tally("ssm_turned", C)
        xst_done = tally("xst_done", C)
        conv_done = tally("conv_done", C)
        tanh_done = tally("tanh_done", C)
        xc_done = tally("xc_done", C)
        g_ready = tally("gate_ready", C)
        g_done = tally("gate_done", C)
        gate_kept = tally("gate_kept", 1)
        d_ready = tally("delta_ready", C)
        sp_done = tally("softplus_parts", 1)
        u_done = tally("u_done", 2)
        bc_ready = tally("bc_ready", 1)
        bc_high = tally("bc_high", 1)
        bc_done = tally("bc_done", 1)
        b_ready = tally("b_spread", NS)
        b_done = tally("b_copied", NS)
        dec_ready = tally("decay_ready", NS)
        inp_ready = tally("input_ready", NS)
        scan_done = tally("scan_done", NS, credit=2)
        c_ready = tally("c_spread", NS)
        hc_done = tally("hc_done", NS, credit=1)
        y_added = tally("y_added", NS - 1, credit=2)
        yg_done = tally("gated_y", 1)
        so_ready = tally("ssm_out_ready", 2)
        x3_done = tally("x3_done", 2)
        dve_a = tally("dve_attn_steps", 3)
        dve_m = tally("dve_max_steps", 1)
        dve_h = tally("dve_head_steps", H // HG)
        dve_n = [tally(f"dve_normalise_steps{k}", 3) for k in range(3)]
        dve_r = [tally(f"dve_router_steps{f}", 11) for f in range(2)]
        dve_s = tally("dve_ssm_steps", TAPS - 1 + 2)
        act_s = tally("act_ssm_steps", 2)

        block = ctx.enter_context(nc.Block())

        def rows(t, n=TB):
            return t[:, None, :].to_broadcast([P, n, D])

        N_LOADS = 24
        M_EARLY = 8
        MAX_BANK = [(0, 1)[g % 2] if g < M_EARLY else (3, 2, 6, 7)[g % 4] for g in range(HP * UN)]
        B_DVE = (5, 6, 7, 8, 9, 10, 11)
        SCORE_BANK = (0, 1, 3, 6)
        PV_BANK = (4, 7)
        QK_BANK = (6, 7, 2, 3)
        V_BANK = (4, 6)
        DT_BANK = (6, 7)
        H_STEP = {1: 4, 2: 5, 4: 6, 5: 7, 6: 8}

        @block.sync
        def _(sp):
            def chunked(w):
                return w.rearrange("(c p) n -> p c n", p=P)

            def load_x(b):
                sp.wait_ge(x_used.sem, x_used.at(b, 0))
                sp.dma_start(x_in[:, :, :], x[b].rearrange("(t p) d -> p t d", p=P)).then_inc(x_loaded.sem, 16)

            loads = [
                (w_row[:, :], norm_w[None, :].to_broadcast([P, D])),
                (wqk[:, :, :], chunked(wqk_t)), (bqk[:, :], bqk_c), (wv[:, :, :], chunked(wv_t)),
                (bv_row[:, :], bv[None, :].to_broadcast([P, D])), (bo_row[:, :], bo[None, :].to_broadcast([P, D])),
                (a_neg[:, :, :], chunked(log_a)), (bg_c[:, :], bg), (cw[:, :, :], chunked(conv_w)),
                (cb[:, :], conv_b), (wso[:, :, :], chunked(wso_t)), (wo[:, :, :], chunked(wo_t)),
                (wd[:, :, :], chunked(wd_t)), (wg[:, :, :], chunked(wg_t)),
                (wbase[:, :, :], chunked(base_t)), (wdown[:, :, :], chunked(down_t)), (wup[0:(E + 1) * R, :], up_s),
                (bd_c[:, :], bd), (bso_row[:, :], bso[None, :].to_broadcast([P, D])),
                (wup[(E + 1) * R:, :], base_b[None, :]),
                (rb_row[:, :], router_b[None, :].to_broadcast([P, E])),
            ]
            loads += [(wbc[:, :, j, :], chunked(wbc_t)) for j in range(3)]
            assert len(loads) == N_LOADS

            def max_rows(b):
                sp.wait_ge(mrow_done.sem, mrow_done.at(b, 1))
                for r in range(2):
                    sp.dma_start(sq[KS + r:KS + r + 1, :, :], mrow[:, r, :]).then_inc(m_stacked.sem, 16)

            def stack(b):
                for j, made in enumerate((qk_biased, mid_done, low_done)):
                    sp.wait_ge(made.sem, made.at(b, made.per))
                    sp.dma_start(scratch[b, j].rearrange("g p t -> p g t"),
                                 parts[:, j, :, :]).then_inc(part_stored.sem, 16)
                sp.wait_ge(part_stored.sem, part_stored.at(b, 3))
                for s, (jq, jk) in enumerate(TERMS):
                    for dst, j, g in ((sq, jq, 0), (sk, jk, C)):
                        src = scratch[b, j, g:g + C].rearrange("g (h i) t -> i (g h) t", i=HD)
                        sp.dma_start(dst[s * HD:(s + 1) * HD, :, :], src).then_inc(stacked.sem, 16)

            def store(b):
                sp.wait_ge(f_done[1].sem, f_done[1].at(b, 2))
                sp.dma_start(out[b].rearrange("(t p) d -> p t d", p=P), x_out[:, :, :]).then_inc(x_stored.sem, 16)

            load_x(0)
            for dst, src in loads:
                sp.dma_start(dst, src).then_inc(w_in, 16)
            sp.sem_inc(x_stored.sem, 16)
            stack(0)
            for i in range(2):
                max_rows(i)
                load_x(i + 1)
                stack(i + 1)
            with sp.Fori(2, NB - 1) as i:
                store(i - 2)
                max_rows(i)
                load_x(i + 1)
                stack(i + 1)
            store(NB - 3)
            max_rows(NB - 1)
            store(NB - 2)
            store(NB - 1)
            sp.wait_ge(x_stored.sem, 16 * (NB + 1))

        @block.tensor
        def _(pe):
            mm = nc.tensor.matmul

            def turn(src, dst, c):
                for tb in range(TB):
                    last = nc.tensor.transpose(dst[:, tb * P:(tb + 1) * P], src[:, tb, c * P:(c + 1) * P],
                                               ident[:, :])
                return last

            def by_columns(dst, w, src, g):
                for c in range(C):
                    last = mm(dst, w[:, c, g * P:(g + 1) * P], src[:, c, :], start=(c == 0), stop=(c == C - 1))
                return last

            def by_tokens(dst, src, w, j):
                for tb in (2 * j, 2 * j + 1):
                    o = (tb % 2) * D
                    for c in range(C):
                        last = mm(dst[:, o:o + D], src[:, c, tb * P:(tb + 1) * P], w[:, c, :],
                                  start=(c == 0), stop=(c == C - 1))
                return last

            def turn_xn(b):
                pe.wait_ge(xn_done.sem, xn_done.at(b, 1))
                pe.wait_ge(mx_used.sem, mx_used.at(b, 0))
                for c in range(C):
                    turn(xn, bank[2 + c], c).then_inc(xn_turned.sem, 1)

            def project_qk(b, first, end):
                if first == 0:
                    pe.wait_ge(xnt_done.sem, xnt_done.at(b, C))
                for g in range(first, end):
                    by_columns(bank[QK_BANK[g]][:, :], wqk, xt_b, g).then_inc(qk_ready.sem, 1)

            def project_v(b, j):
                pe.wait_ge(qk_biased.sem, qk_biased.at(b, 1))
                by_tokens(bank[V_BANK[j]], xt_b, wv, j).then_inc(v_ready.sem, 1)

            def max_block(dst, h, qb, o):
                n = (qb + 1) * P
                mm(dst[:, o:o + n], sq[0:KS, h, qb * P:(qb + 1) * P], sk[0:KS, h, 0:n], start=True, stop=False)
                return mm(dst[:, o + n - P:o + n], ident_bf[:, :], mask_qk[:, :], start=False, stop=True)

            def max_unit(b, g):
                j, un = divmod(g, UN)
                if g == 0:
                    pe.wait_ge(stacked.sem, stacked.at(b, 2 * len(TERMS)))
                pe.wait_ge(mx_used.sem, mx_used.at(b, g - 1 if g < M_EARLY else g - 3))
                dst = bank[MAX_BANK[g]]
                h = 2 * j + un // 2
                if un == 4:
                    max_block(dst, 2 * j, 1, 0)
                    last = max_block(dst, 2 * j + 1, 1, 2 * P)
                elif un % 2 == 0:
                    last = max_block(dst, h, 3, 0)
                else:
                    max_block(dst, h, 2, 0)
                    last = max_block(dst, h, 0, 3 * P)
                last.then_inc(mx_ready.sem, 1)

            def max_rows(b):
                pe.wait_ge(negm_done.sem, negm_done.at(b, 1))
                for qb in range(TB):
                    last = nc.tensor.transpose(bank[2][0:H, qb * P:(qb + 1) * P], negm[:, qb, :], ident[:, :])
                last.then_inc(mx_ready.sem, 1)

            def score_block(dst, h, kb, o):
                n = T - kb * P
                mm(dst[:, o:o + n], sk[:, h, kb * P:(kb + 1) * P], sq[:, h, kb * P:T], start=True, stop=False)
                return mm(dst[:, o:o + P], ident_bf[:, :], mask_kq[:, :], start=False, stop=True)

            def score_unit(b, g):
                j, un = divmod(g, UN)
                if g == 0:
                    pe.wait_ge(m_stacked.sem, m_stacked.at(b, 2))
                pe.wait_ge(exp_done.sem, exp_done.at(b, g - 3))
                dst = bank[SCORE_BANK[g % 4]]
                h = 2 * j + un // 2
                if un == 4:
                    score_block(dst, 2 * j, 2, 0)
                    last = score_block(dst, 2 * j + 1, 2, 2 * P)
                elif un % 2 == 0:
                    last = score_block(dst, h, 0, 0)
                else:
                    score_block(dst, h, 1, 0)
                    last = score_block(dst, h, 3, 3 * P)
                last.then_inc(st_ready.sem, 1)

            def values(b, j, unit, hh, blocks):
                pe.wait_ge(exp_done.sem, exp_done.at(b, UN * j + unit + 1))
                if unit == 0 and j % 2 == 0 and j >= 4:
                    pe.wait_ge(ot_done.sem, ot_done.at(b, j // 2 - 1))
                r = VW * ((2 * j + hh) % HG)
                for kb in blocks:
                    un, o = ((2 * hh, 0), (2 * hh + 1, 0), (4, hh * 2 * P), (2 * hh + 1, 3 * P))[kb]
                    last = mm(bank[PV_BANK[j // 2 % 2]][r:r + VW, kb * P:T], v_sb[:, kb, 2 * j + hh, :],
                              pt_v[:, j % 2, un, o:o + T - kb * P], start=(kb == 0), stop=(kb == 2))
                return last

            def turn_heads(b, g):
                pe.wait_ge(ot_done.sem, ot_done.at(b, g + 1))
                if g:
                    pe.wait_ge(pv_used.sem, pv_used.at(b, g))
                for qb in range(TB):
                    last = nc.tensor.transpose(bank[2][:, qb * P:(qb + 1) * P], ot_sb[:, qb * P:(qb + 1) * P],
                                               ident[:, :])
                last.then_inc(pv_ready.sem, 1)

            def turn_ao(b):
                pe.wait_ge(pv_used.sem, pv_used.at(b, H // HG))
                for c in range(C):
                    turn(ao, bank[c], c).then_inc(ao_turned.sem, 1)

            def attn_out(b):
                pe.wait_ge(aot_done.sem, aot_done.at(b, C))
                for j in range(2):
                    by_tokens(bank[j], xt_a, wo, j).then_inc(wo_ready.sem, 1)

            def ffn_turn(b, f):
                pe.wait_ge(xhat_f[f].sem, xhat_f[f].at(b, 1))
                for c in range(C):
                    turn(FFN[f][0], bank[c], c).then_inc(f_turned[f].sem, 1)

            def ffn_low(b, f):
                pe.wait_ge(ft_done[f].sem, ft_done[f].at(b, C))
                for tb in range(TB):
                    for c in range(C):
                        last = mm(bank[0][:, tb * LR:(tb + 1) * LR], FFN[f][1][:, c, tb * P:(tb + 1) * P],
                                  wdown[:, c, :], start=(c == 0), stop=(c == C - 1))
                last.then_inc(low_ready[f].sem, 1)

            def ffn_base(f, tb):
                o = (tb % 2) * D
                for c in range(C):
                    mm(bank[FFN[f][2][tb // 2]][:, o:o + D], FFN[f][1][:, c, tb * P:(tb + 1) * P], wbase[:, c, :],
                       start=(c == 0 and tb % 2 == 0), stop=False, skip_group_check=True)

            def ffn_weighted(b, f):
                pe.wait_ge(hw_done[f].sem, hw_done[f].at(b, 1))
                for tb in range(TB):
                    last = nc.tensor.transpose(bank[0][0:(E + 1) * R + 1, tb * P:(tb + 1) * P], hw[:, tb, :],
                                               ident[:, :])
                last.then_inc(hw_turned[f].sem, 1)

            def ffn_up(b, f):
                pe.wait_ge(hwt_done[f].sem, hwt_done[f].at(b, 1))
                for j in range(2):
                    for tb in (2 * j, 2 * j + 1):
                        o = (tb % 2) * D
                        last = mm(bank[FFN[f][2][j]][:, o:o + D], hw_t[:, tb * P:(tb + 1) * P], wup[:, :],
                                  start=False, stop=True, skip_group_check=True)
                    last.then_inc(f_ready[f].sem, 1)

            def ssm_turn(b):
                pe.wait_ge(xhat_s.sem, xhat_s.at(b, 1))
                for c in range(C):
                    turn(tok, bank[c], c).then_inc(s_turned.sem, 1)

            def ssm_gate(b):
                pe.wait_ge(xst_done.sem, xst_done.at(b, C))
                for g in range(C):
                    by_columns(bank[3 + g][:, :], wg, xs_t[:, :, TAPS - 1:], g).then_inc(g_ready.sem, 1)

            def ssm_project(b):
                pe.wait_ge(xc_done.sem, xc_done.at(b, C))
                for c in range(C):
                    last = mm(bank[2][0:6 * NS, :], wbc[:, c, :, :], xc[:, c, :], start=(c == 0), stop=(c == C - 1))
                last.then_inc(bc_ready.sem, 1)
                for g in range(C):
                    by_columns(bank[DT_BANK[g]][:, :], wd, xc, g).then_inc(d_ready.sem, 1)

            def spread_b(b, n):
                if n == 0:
                    pe.wait_ge(hc_done.sem, hc_done.at(b, 0))
                elif n <= LEAD:
                    pe.wait_ge(b_done.sem, b_done.at(b, n))
                else:
                    pe.wait_ge(hc_done.sem, hc_done.at(b, n - LEAD))
                mm(bank[5][:, :], onehot[:, n, :], bcs[:, :], start=True, stop=True).then_inc(b_ready.sem, 1)

            def spread_c(b, n):
                if n + LEAD < NS:
                    pe.wait_ge(b_done.sem, b_done.at(b, n + LEAD + 1))
                else:
                    pe.wait_ge(hc_done.sem, hc_done.at(b, n))
                mm(bank[5][:, :], onehot[:, NS + n, :], bcs[:, :], start=True, stop=True).then_inc(c_ready.sem, 1)

            def ssm_out(b, j):
                pe.wait_ge(yg_done.sem, yg_done.at(b, 1))
                by_tokens(bank[j], gate_y, wso, j).then_inc(so_ready.sem, 1)

            def early_maxima(b, first, end):
                for g in range(first, end):
                    max_unit(b, g)

            def work(i, attn, ssm, late, ahead):
                def ahead_b(k):
                    if ssm:
                        spread_b(i - 1, k + LEAD)

                def step_c(k):
                    if ssm:
                        spread_c(i - 1, k)

                def maxima(first, end):
                    for g in range(first, end) if attn else ():
                        max_unit(i, g)

                if ssm:
                    pe.wait_ge(g_done.sem, g_done.at(i - 1, C))
                maxima(M_EARLY, M_EARLY + 1)
                if ssm:
                    pe.wait_ge(bc_done.sem, bc_done.at(i - 1, 1))
                    spread_b(i - 1, 0)
                maxima(M_EARLY + 1, M_EARLY + 2)
                if ssm:
                    pe.wait_ge(act_s.sem, act_s.at(i - 1, 1))
                maxima(M_EARLY + 2, M_EARLY + 4)
                if ssm:
                    spread_b(i - 1, 1)
                if late:
                    ssm_out(i - 2, 0)
                ahead_b(0)
                maxima(M_EARLY + 4, M_EARLY + 5)
                if late:
                    ssm_out(i - 2, 1)
                maxima(M_EARLY + 5, 14)
                step_c(0)
                maxima(14, 17)
                if late:
                    ffn_turn(i - 2, 1)
                maxima(17, 18)
                ahead_b(1)
                if late:
                    ffn_low(i - 2, 1)
                step_c(1)
                for tb in range(TB):
                    maxima(18 + tb, 19 + tb)
                    if late:
                        ffn_base(1, tb)
                maxima(22, 26)
                if late:
                    ffn_weighted(i - 2, 1)
                maxima(26, 32)
                if late:
                    ffn_up(i - 2, 1)
                maxima(32, 40)
                if attn:
                    max_rows(i)
                ahead_b(2)
                if attn and late:
                    pe.wait_ge(f_done[1].sem, f_done[1].at(i - 2, 2))
                step_c(2)
                ahead_b(3)
                if attn:
                    for un in range(4):
                        score_unit(i, un)
                step_c(3)
                for j in range(HP):
                    def next_scores(un):
                        if attn and j + 1 < HP:
                            score_unit(i, UN * (j + 1) + un)

                    if attn:
                        score_unit(i, UN * j + 4)
                        values(i, j, 0, 0, (0,))
                        next_scores(0)
                        values(i, j, 1, 0, (1, 3))
                        next_scores(1)
                        values(i, j, 2, 1, (0,))
                        next_scores(2)
                    if j in H_STEP:
                        ahead_b(H_STEP[j])
                    if attn:
                        values(i, j, 3, 1, (1, 3))
                        next_scores(3)
                    if j in H_STEP:
                        step_c(H_STEP[j])
                    if attn:
                        values(i, j, 4, 0, (2,))
                        values(i, j, 4, 1, (2,)).then_inc(pt_read.sem, 1)
                        if j % 2 == 1 and j > 1:
                            turn_heads(i, j // 2 - 1)
                ahead_b(9)
                if attn:
                    turn_heads(i, H // HG - 1)
                    turn_ao(i)
                step_c(9)
                if ahead:
                    turn_xn(i + 1)
                if attn:
                    attn_out(i)
                ahead_b(10)
                if ahead:
                    project_qk(i + 1, 0, C)
                step_c(10)
                if attn:
                    ffn_turn(i, 0)
                ahead_b(11)
                if attn:
                    ffn_low(i, 0)
                step_c(11)
                if ahead:
                    project_qk(i + 1, C, 2 * C)
                ahead_b(12)
                if attn:
                    if ahead:
                        pe.wait_ge(qk_biased.sem, qk_biased.at(i + 1, 2))
                    for tb in range(TB):
                        ffn_base(0, tb)
                step_c(12)
                if attn:
                    ffn_weighted(i, 0)
                    ffn_up(i, 0)
                ahead_b(13)
                if ahead:
                    project_v(i + 1, 0)
                step_c(13)
                if ahead:
                    project_v(i + 1, 1)
                if attn:
                    ssm_turn(i)
                    if ahead:
                        pe.wait_ge(v_done.sem, v_done.at(i + 1, 2))
                        pe.wait_ge(qk_biased.sem, qk_biased.at(i + 1, 2 * C))
                    ssm_gate(i)
                step_c(14)
                if ahead:
                    early_maxima(i + 1, 0, 2)
                step_c(15)
                if ahead:
                    early_maxima(i + 1, 2, 4)
                if attn:
                    ssm_project(i)
                if ahead:
                    early_maxima(i + 1, 4, M_EARLY)

            for _n in range(2):
                pe.sem_inc(pt_read.sem, 1)
            pe.wait_ge(w_in, 16 * N_LOADS)
            pe.wait_ge(pool_const, 1)
            pe.wait_ge(dve_const, 1)
            turn_xn(0)
            project_qk(0, 0, 2 * C)
            project_v(0, 0)
            project_v(0, 1)
            early_maxima(0, 0, M_EARLY)
            work(0, True, False, False, True)
            work(1, True, True, False, True)
            with pe.Fori(2, NB - 1) as i:
                work(i, True, True, True, True)
            work(NB - 1, True, True, True, False)
            work(NB, False, True, True, False)
            work(NB + 1, False, False, True, False)

        @block.scalar
        def _(act):
            A = nc.scalar.activation

            def copies(b, ready, done, bank0, dst):
                for c in range(C):
                    act.wait_ge(ready.sem, ready.at(b, c + 1))
                    nc.scalar.copy(dst[:, c, :], bank[bank0 + c][:, :]).then_inc(done.sem, 1)

            def split_qk(b, first, end):
                for g in range(first, end):
                    act.wait_ge(qk_ready.sem, qk_ready.at(b, g + 1))
                    scale = HD ** -0.5 if g < C else 1.0
                    A(qkf[:, g, :], bank[QK_BANK[g]][:, :], ACT.Identity, bias=bqk[:, g:g + 1], scale=scale)
                    A(parts[:, 0, g, :], bank[QK_BANK[g]][:, :], ACT.Identity, bias=bqk[:, g:g + 1],
                      scale=scale).then_inc(qk_biased.sem, 1)

            def split_mid(b):
                for j in range(2):
                    act.wait_ge(high_off.sem, high_off.at(b, j + 1))
                    nc.scalar.copy(parts[:, 1, C * j:C * j + C, :], qkf[:, C * j:C * j + C, :]).then_inc(mid_done.sem, 1)

            def exp_unit(b, g):
                j, un = divmod(g, UN)
                if un == 0:
                    act.wait_ge(pt_read.sem, pt_read.at(b, j - 1))
                act.wait_ge(st_ready.sem, st_ready.at(b, g + 1))
                A(pt_v[:, j % 2, un, :], bank[SCORE_BANK[g % 4]][:, :], ACT.Exp).then_inc(exp_done.sem, 1)

            def ffn_exp(b, f):
                act.wait_ge(lg_done[f].sem, lg_done[f].at(b, 1))
                A(ex[:, :, :], lg[:, :, :], ACT.Exp).then_inc(ex_done[f].sem, 1)

            def ffn_turned(b, f):
                act.wait_ge(hw_turned[f].sem, hw_turned[f].at(b, 1))
                nc.scalar.copy(hw_t, bank[0][0:(E + 1) * R + 1, :]).then_inc(hwt_done[f].sem, 1)

            def keep_gate(b, late):
                if late:
                    act.wait_ge(so_ready.sem, so_ready.at(b - 1, 2))
                A(gate_y[:, :, :], gate[:, :, :], ACT.Identity, bias=1.0).then_inc(gate_kept.sem, 1)

            def ssm_tanh(b):
                for c in range(C):
                    act.wait_ge(g_ready.sem, g_ready.at(b, c + 1))
                    A(gate[:, c, :], bank[3 + c][:, :], ACT.Tanh, bias=bg_c[:, c:c + 1], scale=0.5).then_inc(g_done.sem, 1)
                for c in range(C):
                    act.wait_ge(conv_done.sem, conv_done.at(b, c + 1))
                    A(sp_t[:, c, :], xc[:, c, :], ACT.Tanh).then_inc(tanh_done.sem, 1)

            def ssm_softplus(b, ssm):
                act.wait_ge(bc_ready.sem, bc_ready.at(b, 1))
                if ssm:
                    act.wait_ge(c_ready.sem, c_ready.at(b - 1, NS))
                nc.scalar.copy(bcs[:, :], bank[2][0:6 * NS, :]).then_inc(bc_high.sem, 1)
                for c, src in enumerate((bank[DT_BANK[0]], bank[DT_BANK[1]])):
                    act.wait_ge(d_ready.sem, d_ready.at(b, c + 1))
                    A(dt[:, c, :], src[:, :], ACT.Relu, bias=bd_c[:, c:c + 1])
                    last = A(sp_t[:, c, :], src[:, :], ACT.Abs, bias=bd_c[:, c:c + 1])
                last.then_inc(act_s.sem, 1)
                act.wait_ge(act_s.sem, act_s.next(b))
                A(sp_t[:, :, :], sp_t[:, :, :], ACT.Exp, scale=-1.0).then_inc(act_s.sem, 1)
                act.wait_ge(act_s.sem, act_s.next(b))
                A(sp_t[:, :, :], sp_t[:, :, :], ACT.Ln, bias=1.0).then_inc(sp_done.sem, 1)

            def copy_b(b, n):
                act.wait_ge(b_ready.sem, b_ready.at(b, n + 1))
                if n >= RB:
                    act.wait_ge(inp_ready.sem, inp_ready.at(b, n - RB + 1))
                nc.scalar.copy(b_all[:, n % RB, :], bank[5][:, :]).then_inc(b_done.sem, 1)

            def decays(b, n):
                if n == 0:
                    act.wait_ge(u_done.sem, u_done.at(b, 1))
                act.wait_ge(scan_done.sem, scan_done.at(b, n - 1))
                for c in range(C):
                    last = A(dec[:, n % 2, c, 1:T], dt[:, c, 1:T], ACT.Exp, scale=a_neg[:, c, n:n + 1])
                last.then_inc(dec_ready.sem, 1)

            def step(b, k):
                if k + LEAD < NS and k + LEAD not in B_DVE:
                    copy_b(b, k + LEAD)
                if k + 1 < NS:
                    decays(b, k + 1)

            def work(i, attn, ssm, late, ahead):
                if ssm:
                    for n in range(LEAD):
                        copy_b(i - 1, n)
                    decays(i - 1, 0)
                    step(i - 1, 0)
                if late:
                    copies(i - 2, f_turned[1], ft_done[1], 0, xt_b)
                if ssm:
                    step(i - 1, 1)
                if late:
                    ffn_exp(i - 2, 1)
                    ffn_turned(i - 2, 1)
                if ssm:
                    step(i - 1, 2)
                    step(i - 1, 3)
                for j in range(HP):
                    if attn:
                        for un in range(UN):
                            exp_unit(i, UN * j + un)
                    if ssm and j in H_STEP:
                        step(i - 1, H_STEP[j])
                if attn:
                    copies(i, ao_turned, aot_done, 0, xt_a)
                if ssm:
                    step(i - 1, 9)
                if ahead:
                    copies(i + 1, xn_turned, xnt_done, 2, xt_b)
                if ahead:
                    split_qk(i + 1, 0, C)
                if ssm:
                    step(i - 1, 10)
                if attn:
                    copies(i, f_turned[0], ft_done[0], 0, xt_a)
                if ssm:
                    step(i - 1, 11)
                if attn:
                    ffn_exp(i, 0)
                if ahead:
                    split_qk(i + 1, C, 2 * C)
                if ssm:
                    step(i - 1, 12)
                if attn:
                    ffn_turned(i, 0)
                if ahead:
                    split_mid(i + 1)
                if ssm:
                    step(i - 1, 13)
                if attn:
                    copies(i, s_turned, xst_done, 0, xs_t[:, :, TAPS - 1:])
                if ssm:
                    keep_gate(i - 1, late)
                    step(i - 1, 14)
                    act.wait_ge(gate_kept.sem, gate_kept.at(i - 1, 1))
                if attn:
                    ssm_tanh(i)
                    ssm_softplus(i, ssm)

            for _n in range(4):
                act.sem_inc(exp_done.sem, 1)
            act.wait_ge(w_in, 16 * N_LOADS)
            A(a_neg[:, :, :], a_neg[:, :, :], ACT.Exp).then_inc(act_const, 1)
            act.wait_ge(dve_const, 1)
            copies(0, xn_turned, xnt_done, 2, xt_b)
            split_qk(0, 0, 2 * C)
            split_mid(0)
            work(0, True, False, False, True)
            work(1, True, True, False, True)
            with act.Fori(2, NB - 1) as i:
                work(i, True, True, True, True)
            work(NB - 1, True, True, True, False)
            work(NB, False, True, True, False)
            work(NB + 1, False, False, True, False)

        @block.vector
        def _(dve):
            V = nc.vector

            def moments(b, src, steps, var, mul, add):
                for tb in range(TB):
                    last = V.bn_stats(st[:, tb, :], src[:, tb, :])
                last.then_inc(steps.sem, 1)
                dve.wait_ge(steps.sem, steps.next(b))
                dve.sem_inc(waited, 1)
                for tb in range(TB):
                    last = V.bn_aggr(mv[:, tb, :], st[:, tb, :])
                last.then_inc(steps.sem, 1)
                dve.wait_ge(steps.sem, steps.next(b))
                V.tensor_scalar(va[:, :], mv[:, :, 1], mul, add, ALU.mult, ALU.add).then_inc(var.sem, 1)

            def normalise(b, src, steps, rsq, done, dst):
                dve.wait_ge(rsq.sem, rsq.at(b, 1))
                V.scalar_tensor_tensor(nm[:, :], mv[:, :, 0], -1.0, rs[:, :], ALU.mult, ALU.mult).then_inc(steps.sem, 1)
                dve.wait_ge(steps.sem, steps.next(b))
                for tb in range(TB):
                    last = V.tensor_scalar(dst[:, tb, :], src[:, tb, :], rs[:, tb:tb + 1], nm[:, tb:tb + 1],
                                           ALU.mult, ALU.add)
                last.then_inc(done.sem, 1)

            def attn_moments(b):
                dve.wait_ge(x_loaded.sem, x_loaded.at(b, 1))
                e1, e2 = 1e-5, 1e-6
                moments(b, x_in, dve_a, var_a, 1.0 + e2, e1 * e2)

            def attn_normalise(b):
                normalise(b, x_in, dve_a, rs_a, xhat_a, tok)

            def attn_v(b):
                for j in range(2):
                    dve.wait_ge(v_ready.sem, v_ready.at(b, j + 1))
                    V.tensor_tensor(v_sb[:, 2 * j:2 * j + 2, :, 0:HD],
                                    bank[V_BANK[j]][:, :].rearrange("p (t h i) -> p t h i", t=2, h=H),
                                    rows(bv_row, 2).rearrange("p t (h i) -> p t h i", h=H),
                                    ALU.add).then_inc(v_done.sem, 1)

            def maximum(b, g):
                dve.wait_ge(mx_ready.sem, mx_ready.at(b, g + 1))
                src = bank[MAX_BANK[g]][:, :].rearrange("p (k n) -> p k n", k=TB)
                V.tensor_reduce(mxp[:, g // UN, g % UN, :], src, AXX, ALU.max).then_inc(mx_used.sem, 1)

            def max_columns(b):
                dve.wait_ge(mx_used.sem, mx_used.at(b, HP * UN))

                def neg(qb, src):
                    dst = negm[:, qb, :].rearrange("p (j h) -> p j h", h=2)
                    return V.tensor_reduce(dst, src, AXX, ALU.max, negate=True)

                neg(3, mxp[:, :, 0:3:2, :])
                neg(2, mxp[:, :, 1:4:2, 0:3])
                neg(0, mxp[:, :, 1:4:2, 3:4])
                neg(1, mxp[:, :, 4, :].rearrange("p j (h k) -> p j h k", h=2)).then_inc(negm_done.sem, 1)

            def max_rows(b):
                dve.wait_ge(mx_ready.sem, mx_ready.at(b, HP * UN + 1))
                V.tensor_copy(mrow[:, 0, :], bank[2][0:H, :]).then_inc(dve_m.sem, 1)
                dve.wait_ge(dve_m.sem, dve_m.next(b))
                V.tensor_tensor(mrow[:, 1, :], bank[2][0:H, :], mrow[:, 0, :], ALU.subtract).then_inc(mrow_done.sem, 1)

            def copy_heads(b, g):
                dve.wait_ge(pt_read.sem, pt_read.at(b, HG // 2 * (g + 1)))
                V.tensor_copy(ot_sb[:, :], bank[PV_BANK[g % 2]][:, :]).then_inc(ot_done.sem, 1)

            def head_norm(b, g):
                dve.wait_ge(pv_ready.sem, pv_ready.at(b, g + 1))
                pv = bank[2][:, :].rearrange("p (t h i) -> p t h i", t=TB, h=HG)
                V.reciprocal(rc[:, :, :], pv[:, :, :, HD]).then_inc(dve_h.sem, 1)
                dve.wait_ge(dve_h.sem, dve_h.next(b))
                V.tensor_tensor(ao[:, :, g * HG * HD:(g + 1) * HG * HD].rearrange("p t (h i) -> p t h i", h=HG),
                                pv[:, :, :, 0:HD], rc[:, :, :, None].to_broadcast([P, TB, HG, HD]),
                                ALU.mult).then_inc(pv_used.sem, 1)

            def add_out(b, ready, done, banks, src, dst):
                for j in range(2):
                    dve.wait_ge(ready.sem, ready.at(b, j + 1))
                    V.tensor_tensor(dst[:, 2 * j:2 * j + 2, :],
                                    bank[banks[j]][:, :].rearrange("p (t d) -> p t d", t=2),
                                    src[:, 2 * j:2 * j + 2, :], ALU.add).then_inc(done.sem, 1)

            def ffn_moments(b, f):
                added = (x1_done, x3_done)[f]
                dve.wait_ge(added.sem, added.at(b, 2))
                moments(b, (res_a, x_out)[f], dve_n[f], var_f[f], 1.0, 1e-5)

            def ffn_normalise(b, f):
                normalise(b, (res_a, x_out)[f], dve_n[f], rs_f[f], xhat_f[f], FFN[f][0])

            def router_in(b, f):
                low = bank[0][:, 0:TB * LR].rearrange("p (t l) -> p t l", t=TB)
                steps = dve_r[f]
                dve.wait_ge(low_ready[f].sem, low_ready[f].at(b, 1))
                V.tensor_tensor(lg[:, :, :], low[:, :, LR - E:LR], rb_row[:, None, :].to_broadcast([P, TB, E]),
                                ALU.add).then_inc(steps.sem, 1)
                dve.wait_ge(steps.sem, steps.next(b))
                V.tensor_reduce(red[:, 0, :], lg[:, :, :], AXX, ALU.max).then_inc(steps.sem, 1)
                dve.wait_ge(steps.sem, steps.next(b))
                V.tensor_tensor(lg[:, :, :], lg[:, :, :], red[:, 0, :, None].to_broadcast([P, TB, E]),
                                ALU.subtract).then_inc(lg_done[f].sem, 1)

            def router_out(b, f):
                low = bank[0][:, 0:TB * LR].rearrange("p (t l) -> p t l", t=TB)
                steps = dve_r[f]
                dve.wait_ge(ex_done[f].sem, ex_done[f].at(b, 1))
                mine = ex[:, :, :, None].to_broadcast([P, TB, E, E])
                other = ex[:, :, None, :].to_broadcast([P, TB, E, E])
                V.tensor_tensor(cmp_b[:, :, :, :], other, mine, ALU.is_equal).then_inc(steps.sem, 1)
                V.tensor_tensor(cmp_a[:, :, :, :], other, mine, ALU.is_gt)
                dve.wait_ge(steps.sem, steps.next(b))
                V.tensor_tensor(cmp_b[:, :, :, :], cmp_b[:, :, :, :],
                                below[:, None, :, :].to_broadcast([P, TB, E, E]), ALU.mult).then_inc(steps.sem, 1)
                V.tensor_reduce(red[:, 1, :], ex[:, :, :], AXX, ALU.add)
                dve.wait_ge(steps.sem, steps.next(b))
                V.tensor_tensor(cmp_a[:, :, :, :], cmp_a[:, :, :, :], cmp_b[:, :, :, :],
                                ALU.add).then_inc(steps.sem, 1)
                dve.wait_ge(steps.sem, steps.next(b))
                V.tensor_reduce(rank[:, :, :], cmp_a[:, :, :, :], AXX, ALU.add).then_inc(steps.sem, 1)
                dve.wait_ge(steps.sem, steps.next(b))
                V.scalar_tensor_tensor(rank[:, :, :], rank[:, :, :], 1.5, ex[:, :, :], ALU.is_lt,
                                       ALU.mult).then_inc(steps.sem, 1)
                dve.wait_ge(steps.sem, steps.next(b))
                V.tensor_reduce(red[:, 2, :], rank[:, :, :], AXX, ALU.add).then_inc(steps.sem, 1)
                dve.wait_ge(steps.sem, steps.next(b))
                V.scalar_tensor_tensor(red[:, 3, :], red[:, 1, :], 1e-6, red[:, 2, :], ALU.mult,
                                       ALU.add).then_inc(steps.sem, 1)
                dve.wait_ge(steps.sem, steps.next(b))
                V.reciprocal(red[:, 3, :], red[:, 3, :]).then_inc(steps.sem, 1)
                dve.wait_ge(steps.sem, steps.next(b))
                V.tensor_tensor(wts[:, :, 1:], rank[:, :, :], red[:, 3, :, None].to_broadcast([P, TB, E]),
                                ALU.mult).then_inc(steps.sem, 1)
                dve.wait_ge(steps.sem, steps.next(b))
                V.tensor_tensor(hw[:, :, 0:(E + 1) * R].rearrange("p t (e r) -> p t e r", r=R),
                                low[:, :, 0:(E + 1) * R].rearrange("p t (e r) -> p t e r", r=R),
                                wts[:, :, :, None].to_broadcast([P, TB, E + 1, R]),
                                ALU.mult).then_inc(hw_done[f].sem, 1)

            def ffn_add(b, f):
                if f == 0:
                    add_out(b, f_ready[0], f_done[0], FFN[0][2], res_a, res_a)
                else:
                    add_out(b, f_ready[1], f_done[1], FFN[1][2], x_out, x_out)

            def ssm_moments(b):
                dve.wait_ge(f_done[0].sem, f_done[0].at(b, 2))
                moments(b, res_a, dve_n[2], var_s, 1.0, 1e-5)

            def ssm_normalise(b):
                normalise(b, res_a, dve_n[2], rs_s, xhat_s, tok)

            def ssm_conv(b):
                dve.wait_ge(xst_done.sem, xst_done.at(b, C))
                for k in range(TAPS):
                    for c in range(C):
                        if k == 0:
                            last = V.tensor_scalar(xc[:, c, :], xs_t[:, c, 0:T], cw[:, c, 0:1], cb[:, c:c + 1],
                                                   ALU.mult, ALU.add)
                        else:
                            last = V.scalar_tensor_tensor(xc[:, c, :], xs_t[:, c, k:k + T], cw[:, c, k:k + 1],
                                                          xc[:, c, :], ALU.mult, ALU.add)
                        if k == TAPS - 1:
                            last.then_inc(conv_done.sem, 1)
                    if k < TAPS - 1:
                        last.then_inc(dve_s.sem, 1)
                        dve.wait_ge(dve_s.sem, dve_s.next(b))

            def ssm_silu(b):
                for c in range(C):
                    dve.wait_ge(tanh_done.sem, tanh_done.at(b, c + 1))
                    V.scalar_tensor_tensor(xc[:, c, :], sp_t[:, c, :], 1.0, xc[:, c, :], ALU.add,
                                           ALU.mult).then_inc(xc_done.sem, 1)

            def ssm_bc(b):
                dve.wait_ge(bc_high.sem, bc_high.at(b, 1))
                V.tensor_tensor(bcr[:, :], bank[2][0:6 * NS, :], bcs[:, :], ALU.subtract).then_inc(dve_s.sem, 1)
                dve.wait_ge(dve_s.sem, dve_s.next(b))
                V.tensor_copy(bcs[2 * NS:4 * NS, :], bcr[2 * NS:4 * NS, :])
                V.tensor_copy(bcs[4 * NS:6 * NS, :], bcr[4 * NS:6 * NS, :]).then_inc(dve_s.sem, 1)
                dve.wait_ge(dve_s.sem, dve_s.next(b))
                V.tensor_tensor(bcs[4 * NS:6 * NS, :], bcr[4 * NS:6 * NS, :], bcs[4 * NS:6 * NS, :],
                                ALU.subtract).then_inc(bc_done.sem, 1)

            def scan(b, n):
                dve.wait_ge(dec_ready.sem, dec_ready.at(b, n + 1))
                dve.wait_ge(inp_ready.sem, inp_ready.at(b, n + 1))
                if n == 2:
                    dve.wait_ge(hc_done.sem, hc_done.at(b, 1))
                else:
                    dve.wait_ge(y_added.sem, y_added.at(b, n - 1 if n < 2 else n - 2))
                h, d, u_b = (t[:, n % 2, :, :].rearrange("p c t -> p (c t)") for t in (hc, dec, inp))
                V.tensor_tensor_scan(h, d, u_b, 0.0, ALU.mult, ALU.add).then_inc(scan_done.sem, 1)

            def times_c(b, n):
                dve.wait_ge(scan_done.sem, scan_done.at(b, n + 1))
                dve.wait_ge(c_ready.sem, c_ready.at(b, n + 1))
                dst = hc[:, n % 2, :, :] if n else y_sum[:, :, :]
                V.tensor_tensor(dst, hc[:, n % 2, :, :],
                                bank[5][:, None, :].to_broadcast([P, C, T]), ALU.mult).then_inc(hc_done.sem, 1)

            def split_high(b, j):
                dve.wait_ge(qk_biased.sem, qk_biased.at(b, C * (j + 1)))
                half_qk = qkf[:, C * j:C * j + C, :]
                V.tensor_tensor(half_qk, half_qk, parts[:, 0, C * j:C * j + C, :],
                                ALU.subtract).then_inc(high_off.sem, 1)

            def ssm_step(b):
                dve.wait_ge(sp_done.sem, sp_done.at(b, 1))
                V.tensor_tensor(dt[:, :, :], dt[:, :, :], sp_t[:, :, :], ALU.add).then_inc(u_done.sem, 1)
                dve.wait_ge(u_done.sem, u_done.at(b, 1))
                V.tensor_tensor(u[:, :, :], dt[:, :, :], xc[:, :, :], ALU.mult).then_inc(u_done.sem, 1)

            def copy_b(b, n):
                dve.wait_ge(b_ready.sem, b_ready.at(b, n + 1))
                dve.wait_ge(inp_ready.sem, inp_ready.at(b, n - RB + 1))
                V.tensor_copy(b_all[:, n % RB, :], bank[5][:, :]).then_inc(b_done.sem, 1)

            def step(b, k):
                scan(b, k)
                if k + LEAD in B_DVE:
                    copy_b(b, k + LEAD)
                times_c(b, k)

            def early_maxima(b, first, end):
                for g in range(first, end):
                    maximum(b, g)

            def work(i, attn, ssm, late, ahead):
                def maxima(first, end):
                    for g in range(first, end) if attn else ():
                        maximum(i, g)

                maxima(M_EARLY, M_EARLY + 3)
                if ssm:
                    ssm_step(i - 1)
                maxima(M_EARLY + 3, M_EARLY + 5)
                if late:
                    dve.wait_ge(bias_s.sem, bias_s.at(i - 2, 1))
                    dve.wait_ge(x_stored.sem, x_stored.at(i - 2, 0))
                    add_out(i - 2, so_ready, x3_done, (0, 1), res_s, x_out)
                    ffn_moments(i - 2, 1)
                maxima(M_EARLY + 5, 14)
                if late:
                    ffn_normalise(i - 2, 1)
                if late:
                    dve.wait_ge(yg_done.sem, yg_done.at(i - 2, 1))
                if ssm:
                    step(i - 1, 0)
                maxima(14, 20)
                if late:
                    router_in(i - 2, 1)
                maxima(20, 22)
                if ssm:
                    step(i - 1, 1)
                if late:
                    router_out(i - 2, 1)
                maxima(22, 40)
                if attn:
                    max_columns(i)
                if late:
                    ffn_add(i - 2, 1)
                if attn:
                    max_rows(i)
                if ssm:
                    step(i - 1, 2)
                    step(i - 1, 3)
                for j in range(HP):
                    if attn and j % 2 == 0 and j:
                        copy_heads(i, j // 2 - 1)
                    if ahead and j == 3:
                        attn_moments(i + 1)
                    if ssm and j in H_STEP:
                        step(i - 1, H_STEP[j])
                    if ahead and j == 6:
                        attn_normalise(i + 1)
                    if attn and j % 2 == 1 and j > 1:
                        head_norm(i, j // 2 - 1)
                if attn:
                    copy_heads(i, H // HG - 1)
                    head_norm(i, H // HG - 1)
                if ssm:
                    step(i - 1, 9)
                if attn:
                    dve.wait_ge(res_done.sem, res_done.at(i, 1))
                    add_out(i, wo_ready, x1_done, (0, 1), res_a, res_a)
                    ffn_moments(i, 0)
                if ssm:
                    scan(i - 1, 10)
                if attn:
                    if ahead:
                        dve.wait_ge(xn_done.sem, xn_done.at(i + 1, 1))
                    ffn_normalise(i, 0)
                if ssm:
                    times_c(i - 1, 10)
                if ahead:
                    split_high(i + 1, 0)
                if ssm:
                    scan(i - 1, 11)
                if attn:
                    router_in(i, 0)
                if ssm:
                    times_c(i - 1, 11)
                    scan(i - 1, 12)
                if attn:
                    router_out(i, 0)
                if ahead:
                    split_high(i + 1, 1)
                if ssm:
                    times_c(i - 1, 12)
                    scan(i - 1, 13)
                if attn:
                    ffn_add(i, 0)
                    ssm_moments(i)
                if ssm:
                    times_c(i - 1, 13)
                if attn:
                    ssm_normalise(i)
                if ssm:
                    scan(i - 1, 14)
                if ahead:
                    attn_v(i + 1)
                if attn:
                    ssm_conv(i)
                if ssm:
                    times_c(i - 1, 14)
                if ahead:
                    early_maxima(i + 1, 0, 2)
                if attn:
                    ssm_silu(i)
                if ssm:
                    step(i - 1, 15)
                if ahead:
                    early_maxima(i + 1, 2, 4)
                if attn:
                    ssm_bc(i)
                if ahead:
                    early_maxima(i + 1, 4, M_EARLY)

            V.memset(dec[:, :, :, :], 0.0)
            V.memset(xs_t[:, :, 0:TAPS - 1], 0.0)
            V.memset(v_sb[:, :, :, HD:HD + 1], 1.0)
            V.memset(v_sb[:, :, :, HD + 1:VW], 0.0)
            V.memset(sk[KS:KS + 2, :, :], 1.0)
            V.memset(wts[:, :, :], 1.0)
            V.memset(hw[:, :, (E + 1) * R:], 1.0)
            V.memset(half[:, :], -0.5)
            for _n in range(4):
                dve.sem_inc(mx_used.sem, 1)
            for _n in range(2):
                dve.sem_inc(scan_done.sem, 1)
            dve.sem_inc(hc_done.sem, 1)
            dve.wait_ge(w_in, 16 * N_LOADS)
            dve.wait_ge(act_const, 1)
            dve.wait_ge(pool_const, 1)
            V.tensor_scalar(a_neg[:, :, :], a_neg[:, :, :], -1.0, None, ALU.mult)
            V.tensor_scalar(bqk[:, 0:C], bqk[:, 0:C], HD ** -0.5, None, ALU.mult)
            V.tensor_scalar(bg_c[:, :], bg_c[:, :], 0.5, None, ALU.mult)
            V.tensor_scalar(cb[:, :], cb[:, :], 0.5, None, ALU.mult)
            V.tensor_scalar(cw[:, :, :], cw[:, :, :], 0.5, None, ALU.mult)
            V.tensor_copy(ident_bf[:, :], ident[:, :])
            V.tensor_scalar(wso[:, :, :], wso[:, :, :], 0.5, None, ALU.mult).then_inc(dve_const_step, 1)
            dve.wait_ge(dve_const_step, 1)
            dve.sem_inc(dve_const, 1)
            attn_moments(0)
            attn_normalise(0)
            split_high(0, 0)
            split_high(0, 1)
            attn_v(0)
            early_maxima(0, 0, M_EARLY)
            work(0, True, False, False, True)
            work(1, True, True, False, True)
            with dve.Fori(2, NB - 1) as i:
                work(i, True, True, True, True)
            work(NB - 1, True, True, True, False)
            work(NB, False, True, True, False)
            work(NB + 1, False, False, True, False)

        @block.gpsimd
        def _(pool):
            G = nc.gpsimd

            def rsqrt(b, var, rsq):
                pool.wait_ge(var.sem, var.at(b, 1))
                G.tensor_tensor(rs[:, :], va[:, :], half[:, :], ALU.pow).then_inc(rsq.sem, 1)

            def weigh(b):
                pool.wait_ge(xhat_a.sem, xhat_a.at(b, 1))
                G.tensor_tensor(xn[:, :, :], tok[:, :, :], rows(w_row), ALU.mult).then_inc(xn_done.sem, 1)

            def residual(b):
                pool.wait_ge(xn_done.sem, xn_done.at(b, 1))
                G.tensor_tensor(res_a[:, :, :], x_in[:, :, :], xn[:, :, :], ALU.add).then_inc(x_used.sem, 1)
                pool.wait_ge(x_used.sem, x_used.at(b, 1))
                G.tensor_tensor(res_a[:, :, :], res_a[:, :, :], rows(bo_row), ALU.add).then_inc(res_done.sem, 1)

            def split_low(b):
                for j in range(2):
                    pool.wait_ge(mid_done.sem, mid_done.at(b, j + 1))
                    G.tensor_tensor(parts[:, 2, C * j:C * j + C, :], qkf[:, C * j:C * j + C, :],
                                    parts[:, 1, C * j:C * j + C, :], ALU.subtract).then_inc(low_done.sem, 1)

            def ssm_residual(b, late):
                pool.wait_ge(xhat_s.sem, xhat_s.at(b, 1))
                if late:
                    pool.wait_ge(x3_done.sem, x3_done.at(b - 1, 2))
                G.tensor_tensor(res_s[:, :, :], res_a[:, :, :], rows(bso_row), ALU.add).then_inc(bias_s.sem, 1)
                pool.wait_ge(bias_s.sem, bias_s.at(b, 1))

            def inputs(b, n):
                if n == 0:
                    pool.wait_ge(u_done.sem, u_done.at(b, 2))
                pool.wait_ge(b_done.sem, b_done.at(b, n + 1))
                pool.wait_ge(scan_done.sem, scan_done.at(b, n - 1))
                G.tensor_tensor(inp[:, n % 2, :, :], u[:, :, :],
                                b_all[:, n % RB:n % RB + 1, :].to_broadcast([P, C, T]),
                                ALU.mult).then_inc(inp_ready.sem, 1)

            def gate_out(b):
                pool.wait_ge(gate_kept.sem, gate_kept.at(b, 1))
                pool.wait_ge(y_added.sem, y_added.at(b, NS - 1))
                G.tensor_tensor(gate_y[:, :, :], gate_y[:, :, :], y_sum[:, :, :], ALU.mult).then_inc(yg_done.sem, 1)

            def add_state(b, n):
                pool.wait_ge(hc_done.sem, hc_done.at(b, n + 1))
                if n > 1:
                    pool.wait_ge(y_added.sem, y_added.at(b, n - 1))
                G.tensor_tensor(y_sum[:, :, :], y_sum[:, :, :], hc[:, n % 2, :, :], ALU.add).then_inc(y_added.sem, 1)

            def step(b, k):
                if k + 1 < NS:
                    inputs(b, k + 1)
                if k > 1:
                    add_state(b, k - 1)

            def work(i, attn, ssm, late, ahead):
                if late:
                    rsqrt(i - 2, var_f[1], rs_f[1])
                if ssm:
                    inputs(i - 1, 0)
                    step(i - 1, 0)
                    step(i - 1, 1)
                    ssm_residual(i - 1, late)
                if attn:
                    residual(i)
                if ssm:
                    for k in range(2, 7):
                        step(i - 1, k)
                if ahead:
                    rsqrt(i + 1, var_a, rs_a)
                if ssm:
                    step(i - 1, 7)
                    step(i - 1, 8)
                if ahead:
                    weigh(i + 1)
                if ssm:
                    step(i - 1, 9)
                if attn:
                    rsqrt(i, var_f[0], rs_f[0])
                if ssm:
                    step(i - 1, 10)
                    step(i - 1, 11)
                    step(i - 1, 12)
                if ahead:
                    split_low(i + 1)
                if attn:
                    rsqrt(i, var_s, rs_s)
                if ssm:
                    for k in range(13, NS):
                        step(i - 1, k)
                    add_state(i - 1, NS - 1)
                    gate_out(i - 1)

            G.memset(ident[:, :], 0.0)
            G.memset(mask_qk[:, :], 0.0)
            G.memset(mask_kq[:, :], 0.0)
            G.memset(below[:, :, :], 1.0)
            G.memset(onehot[:, :, :], 0.0).then_inc(pool_const_step, 1)
            pool.wait_ge(pool_const_step, 1)
            G.affine_select(out=ident[:, :], in_=ident[:, :], compare_op=ALU.not_equal, fill=1.0, base=0,
                            pattern=[[-1, P]], channel_multiplier=1)
            G.affine_select(out=mask_qk[:, :], in_=mask_qk[:, :], compare_op=ALU.is_ge, fill=BIG, base=0,
                            pattern=[[-1, P]], channel_multiplier=1)
            G.affine_select(out=mask_kq[:, :], in_=mask_kq[:, :], compare_op=ALU.is_ge, fill=BIG, base=0,
                            pattern=[[1, P]], channel_multiplier=-1)
            G.affine_select(out=below[:, :, :], in_=below[:, :, :], compare_op=ALU.is_gt, fill=0.0, base=0,
                            pattern=[[1, E], [-1, E]], channel_multiplier=0)
            for j in range(3):
                G.affine_select(out=onehot[:, :, :], in_=onehot[:, :, :], compare_op=ALU.not_equal, fill=1.0,
                                base=-2 * NS * j, pattern=[[-1, 2 * NS], [0, P]],
                                channel_multiplier=1).then_inc(pool_const_step, 1)
                pool.wait_ge(pool_const_step, 2 + j)
            pool.sem_inc(pool_const, 1)
            pool.sem_inc(x_used.sem, 1)
            for _n in range(2):
                pool.sem_inc(y_added.sem, 1)
            pool.wait_ge(w_in, 16 * N_LOADS)
            pool.wait_ge(dve_const, 1)
            rsqrt(0, var_a, rs_a)
            weigh(0)
            split_low(0)
            work(0, True, False, False, True)
            work(1, True, True, False, True)
            with pool.Fori(2, NB - 1) as i:
                work(i, True, True, True, True)
            work(NB - 1, True, True, True, False)
            work(NB, False, True, True, False)
            work(NB + 1, False, False, True, False)

        assert all(t.n % t.per == 0 for t in tallies)


def kernel(**inputs):
    import numpy as np
    import concourse.bacc as bacc
    from concourse.bass_utils import run_bass_kernel_spmd

    g = {k: np.asarray(v) for k, v in inputs.items()}
    a, s, f = "L0_attn_a_", "L0_attn_b_", "L0_ffn_"
    E, R, D = g[f + "routed_A"].shape
    t = np.transpose

    def by_partition(*vectors):
        return t(np.concatenate(vectors).reshape(-1, P))

    arrays = {
        "x": g[a + "x"], "norm_w": g[a + "norm_w"],
        "wqk_t": np.concatenate([t(g[a + "Wq"]), t(g[a + "Wk"])], 1), "bqk": by_partition(g[a + "bq"], g[a + "bk"]),
        "wv_t": t(g[a + "Wv"]), "bv": g[a + "bv"], "wo_t": t(g[a + "Wo"]), "bo": g[a + "bo"],
        "conv_w": g[s + "conv_w"][:, 0, :],
        "conv_b": by_partition(g[s + "conv_b"]), "wd_t": t(g[s + "Wd"]), "bd": by_partition(g[s + "bd"]),
        "wbc_t": np.concatenate([t(g[s + "Wb"]), t(g[s + "Wc"])], 1), "log_a": g[s + "log_a"],
        "wg_t": t(g[s + "Wg"]), "bg": by_partition(g[s + "bg"]), "wso_t": t(g[s + "Wo"]), "bso": g[s + "bo"],
        "base_t": t(g[f + "base_W"]), "base_b": g[f + "base_b"],
        "down_t": np.concatenate([t(g[f + "shared_A"]), t(g[f + "routed_A"].reshape(E * R, D)), t(g[f + "router_W"])], 1),
        "up_s": np.concatenate([t(g[f + "shared_B"]), t(g[f + "routed_B"], (0, 2, 1)).reshape(E * R, D)], 0),
        "router_b": g[f + "router_b"],
    }
    arrays = {f"in_{k}": np.ascontiguousarray(v) for k, v in arrays.items()}
    nc = bacc.Bacc("TRN2", target_bir_lowering=False, num_devices=1)
    args = [nc.dram_tensor(k, v.shape, mybir.dt.from_np(v.dtype), kind="ExternalInput").ap() for k, v in arrays.items()]
    out = nc.dram_tensor("out", g[a + "x"].shape, F32, kind="ExternalOutput").ap()
    hybrid_block(nc, *args, out)
    r = run_bass_kernel_spmd(nc, [arrays], core_ids=[0])
    return r.results[0]["out"]
```
